# Optimizing a Trainium2 kernel written in Bass

```python
import numpy as np
import jax
import jax.numpy as jnp

def _softmax(x, axis=-1):
    return jax.nn.softmax(x, axis=axis)

def _gelu(x):
    return jax.nn.gelu(x, approximate=True)

def _silu(x):
    return jax.nn.silu(x)

def _sigmoid(x):
    return jax.nn.sigmoid(x)

def _layernorm(x, axis=-1, eps=1e-05):
    m = jnp.mean(x, axis=axis, keepdims=True)
    v = jnp.var(x, axis=axis, keepdims=True)
    return (x - m) / jnp.sqrt(v + eps)

def _scatter_add(tgt, idx, src, axis=0):
    return tgt.at[idx].add(src)

def _segment_sum(src, seg, n):
    return jax.ops.segment_sum(src, seg, n)
kernel_name = 'mk_xattn_ffn_d2_seqx_r8_c8d6c7'

def setup_inputs(seed: int=0):
    np.random.seed(seed)
    _w = jnp.asarray

    def _rec_inputs():
        import jax
        import jax.numpy as jnp
        _rk = jax.random.key(seed)
        x = -0.0002928 + 1 * jax.random.normal(jax.random.fold_in(_rk, 1), (8, 256, 128), jnp.float32)
        _lenS = 256 - jax.random.randint(jax.random.fold_in(_rk, 7), (8,), 0, max(1, 256 // 4) + 1, jnp.int32)
        _lenS2 = 64 - jax.random.randint(jax.random.fold_in(_rk, 8), (8,), 0, max(1, 64 // 4) + 1, jnp.int32)
        _ctx_1024P = jax.random.normal(jax.random.fold_in(_rk, 11), (8, 16, 128), jnp.float32)
        _ctx_1024c = jax.random.dirichlet(jax.random.fold_in(_rk, 511), 0.3 * jnp.ones((16,), jnp.float32), (8, 64))
        _ctx_1024t = jnp.einsum('bsk,bkd->bsd', _ctx_1024c, _ctx_1024P)
        _ctx_1024t = _ctx_1024t * jax.lax.rsqrt(jnp.mean(jnp.square(_ctx_1024t)) + 1e-12) * 0.953939
        ctx_1024 = -1.39393e-06 + 0.999914 * (_ctx_1024t + 0.3 * jax.random.normal(jax.random.fold_in(_rk, 611), (8, 64, 128), jnp.float32))
        _validS = jnp.arange(256)[None, :] < _lenS[:, None]
        _validS2 = jnp.arange(64)[None, :] < _lenS2[:, None]
        _causal = jnp.tril(jnp.ones((256, 256), dtype=bool))
        mask_Bx1x1xS2_ik0 = jnp.where(jnp.broadcast_to(_validS2[:, None, None, :], (8, 1, 1, 64)), 0, 1).astype(jnp.int32)
        mask_1x1xSxS2_ik0 = jnp.where(jnp.broadcast_to(_validS2[0:1, None, None, :], (1, 1, 256, 64)), 0, 1).astype(jnp.int32)
        return (x, ctx_1024, mask_Bx1x1xS2_ik0, mask_1x1xSxS2_ik0)
    x, ctx_1024, mask_Bx1x1xS2_ik0, mask_1x1xSxS2_ik0 = _rec_inputs()

    def _L0_xattn_setup():
        import jax, jax.numpy as jnp
        import numpy as np
        DIM = 128
        HEADS = 16
        HEAD_DIM = DIM // HEADS
        SCALE = HEAD_DIM ** (-0.5)

        def _split_heads(t):
            b, n, _ = t.shape
            return t.reshape(b, n, HEADS, HEAD_DIM).transpose(0, 2, 1, 3)
        key = jax.random.key(seed)
        ks = jax.random.split(key, 7)
        B, N, M = (2, 256, 256)
        x = jax.random.normal(ks[0], (B, N, DIM), dtype=jnp.float32)
        y = jax.random.normal(ks[1], (B, M, DIM), dtype=jnp.float32)
        s = DIM ** (-0.5)
        Wq = jax.random.normal(ks[2], (DIM, DIM), dtype=jnp.float32) * s
        Wk = jax.random.normal(ks[3], (DIM, DIM), dtype=jnp.float32) * s
        Wv = jax.random.normal(ks[4], (DIM, DIM), dtype=jnp.float32) * s
        Wp = jax.random.normal(ks[5], (DIM, DIM), dtype=jnp.float32) * s
        bp = jax.random.normal(ks[6], (DIM,), dtype=jnp.float32) * 0.01
        return {'x': x, 'y': y, 'Wq': Wq, 'Wk': Wk, 'Wv': Wv, 'Wp': Wp, 'bp': bp}
    _L0_xattn_all = _L0_xattn_setup()
    _L0_xattn_in = {k: v for k, v in _L0_xattn_all.items() if k in ('Wq', 'Wk', 'Wv', 'Wp', 'bp')}
    del _L0_xattn_all

    def _L0_ffn_setup():
        import jax, jax.numpy as jnp
        import numpy as np
        D_MODEL, EXPERT_DIM, NUM_EXPERTS, TOP_K = (128, 256, 16, 2)
        SEQ_LEN, BATCH = (256, 2)
        key = jax.random.key(seed)
        ks = jax.random.split(key, 8)
        s_d = 1.0 / np.sqrt(D_MODEL)
        s_h = 1.0 / np.sqrt(EXPERT_DIM)
        return {'x': jax.random.normal(ks[0], (SEQ_LEN, BATCH, D_MODEL), jnp.float32), 'Wg': jax.random.uniform(ks[1], (D_MODEL, NUM_EXPERTS), jnp.float32, -s_d, s_d), 'bg': jax.random.uniform(ks[2], (NUM_EXPERTS,), jnp.float32, -s_d, s_d), 'bias': jnp.zeros((NUM_EXPERTS,), jnp.float32), 'W1': jax.random.uniform(ks[3], (NUM_EXPERTS, D_MODEL, EXPERT_DIM), jnp.float32, -s_d, s_d), 'b1': jax.random.uniform(ks[4], (NUM_EXPERTS, EXPERT_DIM), jnp.float32, -s_d, s_d), 'W2': jax.random.uniform(ks[5], (NUM_EXPERTS, EXPERT_DIM, D_MODEL), jnp.float32, -s_h, s_h), 'b2': jax.random.uniform(ks[6], (NUM_EXPERTS, D_MODEL), jnp.float32, -s_h, s_h)}
    _L0_ffn_all = _L0_ffn_setup()
    _L0_ffn_in = {k: v for k, v in _L0_ffn_all.items() if k in ('Wg', 'bg', 'bias', 'W1', 'b1', 'W2', 'b2')}
    del _L0_ffn_all

    def _L1_xattn_setup():
        import jax, jax.numpy as jnp
        import numpy as np
        E, H = (128, 16)
        N, S, T = (2, 256, 256)
        key = jax.random.key(seed)
        ks = jax.random.split(key, 8)
        scale = 1.0 / np.sqrt(E)
        q = jax.random.normal(ks[0], (N, S, E), dtype=jnp.float32)
        k = jax.random.normal(ks[1], (N, T, E), dtype=jnp.float32)
        v = jax.random.normal(ks[2], (N, T, E), dtype=jnp.float32)
        pad_mask = jax.random.randint(ks[3], (N, 1, 1, T), 0, 2, dtype=jnp.int32)
        subsq_mask = jnp.tril(jnp.ones((S, T), dtype=jnp.int32))[None, None]
        Wq = jax.random.normal(ks[4], (E, E), dtype=jnp.float32) * scale
        Wk = jax.random.normal(ks[5], (E, E), dtype=jnp.float32) * scale
        Wv = jax.random.normal(ks[6], (E, E), dtype=jnp.float32) * scale
        bq = jnp.zeros((E,), dtype=jnp.float32)
        bk = jnp.zeros((E,), dtype=jnp.float32)
        bv = jnp.zeros((E,), dtype=jnp.float32)
        return {'query': q, 'key': k, 'value': v, 'pad_mask': pad_mask, 'subsq_mask': subsq_mask, 'Wq': Wq, 'bq': bq, 'Wk': Wk, 'bk': bk, 'Wv': Wv, 'bv': bv}
    _L1_xattn_all = _L1_xattn_setup()
    _L1_xattn_in = {k: v for k, v in _L1_xattn_all.items() if k in ('Wq', 'bq', 'Wk', 'bk', 'Wv', 'bv')}
    del _L1_xattn_all

    def _L1_ffn_setup():
        import jax, jax.numpy as jnp
        import numpy as np
        E = 8
        TOP_K = 2
        B, S, D = (2, 512, 128)
        H = 512
        CAPACITY = 256

        def _moe(x, Wg, W1, b1, W2, b2):
            b, s, d = x.shape
            xf = x.reshape(b * s, d)
            logits = xf.astype(jnp.float32) @ Wg.astype(jnp.float32)
            probs = jax.nn.softmax(logits, axis=-1)
            vals, idx = jax.lax.top_k(probs, TOP_K)
            w = vals / (jnp.sum(vals, axis=-1, keepdims=True) + 1e-09)
            counts = jnp.zeros((E,), dtype=jnp.int32)
            combine = jnp.zeros((b * s, E), dtype=jnp.float32)
            for k in range(TOP_K):
                oh = jax.nn.one_hot(idx[:, k], E, dtype=jnp.int32)
                pos = jnp.cumsum(oh, axis=0) - 1 + counts[None, :]
                keep = (oh == 1) & (pos < CAPACITY)
                counts = counts + jnp.sum(keep.astype(jnp.int32), axis=0)
                combine = combine + w[:, k][:, None] * keep.astype(jnp.float32)
            out = jnp.zeros_like(xf)
            for e in range(E):
                h = jax.nn.gelu(xf @ W1[e] + b1[e])
                ye = h @ W2[e] + b2[e]
                out = out + combine[:, e][:, None].astype(xf.dtype) * ye
            return out.reshape(b, s, d)
        key = jax.random.key(seed)
        k0, k1, k2, k3 = jax.random.split(key, 4)
        return {'x': jax.random.normal(k0, (B, S, D), dtype=jnp.float32), 'Wg': jax.random.normal(k1, (D, E), dtype=jnp.float32) * 0.02, 'W1': jax.random.normal(k2, (E, D, H), dtype=jnp.float32) * 0.02, 'b1': jnp.zeros((E, H), dtype=jnp.float32), 'W2': jax.random.normal(k3, (E, H, D), dtype=jnp.float32) * 0.02, 'b2': jnp.zeros((E, D), dtype=jnp.float32)}
    _L1_ffn_all = _L1_ffn_setup()
    _L1_ffn_in = {k: v for k, v in _L1_ffn_all.items() if k in ('Wg', 'W1', 'b1', 'W2', 'b2')}
    del _L1_ffn_all
    return {'x': x, 'ctx_1024': ctx_1024, 'mask_Bx1x1xS2_ik0': mask_Bx1x1xS2_ik0, 'mask_1x1xSxS2_ik0': mask_1x1xSxS2_ik0, 'L0_xattn_Wq': _L0_xattn_in['Wq'], 'L0_xattn_Wk': _L0_xattn_in['Wk'], 'L0_xattn_Wv': _L0_xattn_in['Wv'], 'L0_xattn_Wp': _L0_xattn_in['Wp'], 'L0_xattn_bp': _L0_xattn_in['bp'], 'L0_ffn_Wg': _L0_ffn_in['Wg'], 'L0_ffn_bg': _L0_ffn_in['bg'], 'L0_ffn_bias': _L0_ffn_in['bias'], 'L0_ffn_W1': _L0_ffn_in['W1'], 'L0_ffn_b1': _L0_ffn_in['b1'], 'L0_ffn_W2': _L0_ffn_in['W2'], 'L0_ffn_b2': _L0_ffn_in['b2'], 'L1_xattn_Wq': _L1_xattn_in['Wq'], 'L1_xattn_bq': _L1_xattn_in['bq'], 'L1_xattn_Wk': _L1_xattn_in['Wk'], 'L1_xattn_bk': _L1_xattn_in['bk'], 'L1_xattn_Wv': _L1_xattn_in['Wv'], 'L1_xattn_bv': _L1_xattn_in['bv'], 'L1_ffn_Wg': _L1_ffn_in['Wg'], 'L1_ffn_W1': _L1_ffn_in['W1'], 'L1_ffn_b1': _L1_ffn_in['b1'], 'L1_ffn_W2': _L1_ffn_in['W2'], 'L1_ffn_b2': _L1_ffn_in['b2']}

def reference(x, ctx_1024, mask_Bx1x1xS2_ik0, mask_1x1xSxS2_ik0, L0_xattn_Wq, L0_xattn_Wk, L0_xattn_Wv, L0_xattn_Wp, L0_xattn_bp, L0_ffn_Wg, L0_ffn_bg, L0_ffn_bias, L0_ffn_W1, L0_ffn_b1, L0_ffn_W2, L0_ffn_b2, L1_xattn_Wq, L1_xattn_bq, L1_xattn_Wk, L1_xattn_bk, L1_xattn_Wv, L1_xattn_bv, L1_ffn_Wg, L1_ffn_W1, L1_ffn_b1, L1_ffn_W2, L1_ffn_b2):
    import jax
    import jax.numpy as jnp

    def _L0_xattn_ref(x, y, Wq, Wk, Wv, Wp, bp):
        import jax, jax.numpy as jnp
        import numpy as np
        DIM = 128
        HEADS = 16
        HEAD_DIM = DIM // HEADS
        SCALE = HEAD_DIM ** (-0.5)

        def _split_heads(t):
            b, n, _ = t.shape
            return t.reshape(b, n, HEADS, HEAD_DIM).transpose(0, 2, 1, 3)
        q = _split_heads(x @ Wq)
        k = _split_heads(y @ Wk)
        v = _split_heads(y @ Wv)
        attn = jnp.einsum('bhid,bhjd->bhij', q, k) * SCALE
        attn = jax.nn.softmax(attn, axis=-1)
        out = jnp.einsum('bhij,bhjd->bhid', attn, v)
        b, h, n, d = out.shape
        out = out.transpose(0, 2, 1, 3).reshape(b, n, h * d)
        return out @ Wp + bp

    def _L0_ffn_ref(x, Wg, bg, bias, W1, b1, W2, b2):
        import jax, jax.numpy as jnp
        import numpy as np
        D_MODEL, EXPERT_DIM, NUM_EXPERTS, TOP_K = (128, 256, 16, 2)
        SEQ_LEN, BATCH = (256, 2)
        logits = jnp.einsum('sbd,de->sbe', x, Wg) + bg + bias
        vals, idx = jax.lax.top_k(logits, TOP_K)
        w = jax.nn.softmax(vals - jnp.max(vals, axis=-1, keepdims=True), axis=-1)
        cw = jnp.einsum('sbk,sbke->sbe', w, jax.nn.one_hot(idx, NUM_EXPERTS, dtype=x.dtype))
        h = jax.nn.relu(jnp.einsum('sbd,edh->esbh', x, W1) + b1[:, None, None, :])
        y = jnp.einsum('esbh,ehd->esbd', h, W2) + b2[:, None, None, :]
        out = jnp.einsum('esbd,sbe->sbd', y, cw)
        return out

    def _L1_xattn_ref(query, key, value, pad_mask, subsq_mask, Wq, bq, Wk, bk, Wv, bv):
        import jax, jax.numpy as jnp
        import numpy as np
        E, H = (128, 16)
        N, S, T = (2, 256, 256)
        n, s, e = query.shape
        t = value.shape[1]
        d = e // H
        q = (query @ Wq.T + bq).reshape(n, s, H, d).transpose(0, 2, 1, 3)
        k = (key @ Wk.T + bk).reshape(n, t, H, d).transpose(0, 2, 1, 3)
        v = (value @ Wv.T + bv).reshape(n, t, H, d).transpose(0, 2, 1, 3)
        att = jnp.einsum('bhsd,bhtd->bhst', q, k) / jnp.sqrt(jnp.float32(d))
        att = jnp.where(pad_mask == 0, jnp.float32(-1000000000.0), att)
        att = jnp.where(subsq_mask == 0, jnp.float32(-1000000000.0), att)
        prob = jax.nn.softmax(att, axis=-1)
        out = jnp.einsum('bhst,bhtd->bhsd', prob, v)
        return out.transpose(0, 2, 1, 3).reshape(n, s, e)

    def _L1_ffn_ref(x, Wg, W1, b1, W2, b2):
        import jax, jax.numpy as jnp
        import numpy as np
        E = 8
        TOP_K = 2
        B, S, D = (2, 512, 128)
        H = 512
        CAPACITY = 256

        def _moe(x, Wg, W1, b1, W2, b2):
            b, s, d = x.shape
            xf = x.reshape(b * s, d)
            logits = xf.astype(jnp.float32) @ Wg.astype(jnp.float32)
            probs = jax.nn.softmax(logits, axis=-1)
            vals, idx = jax.lax.top_k(probs, TOP_K)
            w = vals / (jnp.sum(vals, axis=-1, keepdims=True) + 1e-09)
            counts = jnp.zeros((E,), dtype=jnp.int32)
            combine = jnp.zeros((b * s, E), dtype=jnp.float32)
            for k in range(TOP_K):
                oh = jax.nn.one_hot(idx[:, k], E, dtype=jnp.int32)
                pos = jnp.cumsum(oh, axis=0) - 1 + counts[None, :]
                keep = (oh == 1) & (pos < CAPACITY)
                counts = counts + jnp.sum(keep.astype(jnp.int32), axis=0)
                combine = combine + w[:, k][:, None] * keep.astype(jnp.float32)
            out = jnp.zeros_like(xf)
            for e in range(E):
                h = jax.nn.gelu(xf @ W1[e] + b1[e])
                ye = h @ W2[e] + b2[e]
                out = out + combine[:, e][:, None].astype(xf.dtype) * ye
            return out.reshape(b, s, d)
        return _moe(x, Wg, W1, b1, W2, b2)
    x = x + _L0_xattn_ref(_layernorm(x, axis=-1), ctx_1024, L0_xattn_Wq, L0_xattn_Wk, L0_xattn_Wv, L0_xattn_Wp, L0_xattn_bp)
    x = x + _L0_ffn_ref(_layernorm(x, axis=-1), L0_ffn_Wg, L0_ffn_bg, L0_ffn_bias, L0_ffn_W1, L0_ffn_b1, L0_ffn_W2, L0_ffn_b2)
    x = x + _L1_xattn_ref(_layernorm(x, axis=-1), ctx_1024, ctx_1024, mask_Bx1x1xS2_ik0, mask_1x1xSxS2_ik0, L1_xattn_Wq, L1_xattn_bq, L1_xattn_Wk, L1_xattn_bk, L1_xattn_Wv, L1_xattn_bv)
    x = x + _L1_ffn_ref(_layernorm(x, axis=-1), L1_ffn_Wg, L1_ffn_W1, L1_ffn_b1, L1_ffn_W2, L1_ffn_b2)
    return x

_drawn_inputs = setup_inputs


def setup_inputs(seed=0):
    import zlib

    import numpy as np

    out = dict(_drawn_inputs(seed))
    spreads = {'L0_ffn_bias': (0.0, 0.1),
     'L1_xattn_bq': (0.0, 0.387),
     'L1_xattn_bk': (0.0, 0.8),
     'L1_xattn_bv': (0.0, 0.1),
     'L1_ffn_b1': (0.0, 0.8),
     'L1_ffn_b2': (0.0, 0.1)}
    factors = {'L0_xattn_bp': 3.094, 'L0_ffn_b1': 4.27, 'L1_ffn_W1': 2.712}
    for name, (base, spread) in spreads.items():
        noise = np.random.default_rng([zlib.crc32(name.encode()), seed]).standard_normal(out[name].shape)
        drawn = base * np.exp(spread * noise) if base else spread * noise
        out[name] = jnp.asarray(drawn.astype(out[name].dtype))
    for name, factor in factors.items():
        out[name] = (out[name] * factor).astype(out[name].dtype)
    return out
```

```python
from contextlib import ExitStack

import concourse.bass as bass
from concourse import mybir

ALU = mybir.AluOpType
ACT = mybir.ActivationFunctionType
AX = mybir.AxisListType
F32 = mybir.dt.float32
BF16 = mybir.dt.bfloat16
I32 = mybir.dt.int32
U32 = mybir.dt.uint32

P = 128
B, S, D = 8, 256, 128
S2 = 64
H, DH = 16, 8
TOK = B * S
NT = TOK // P
QT = S // P
NC = H // 2
SCALE = DH ** -0.5
EPS = 1e-5
Q_PART = [0, 0, 0, 1, 1, 2]
K_PART = [0, 1, 2, 0, 1, 0]
NP = len(Q_PART)
KR = NP * 2 * DH
MASK = 2.0 ** 100
E0N, F0 = 16, 256
UP0 = TOK
REG0 = 2 * TOK + P
PAD0 = E0N * REG0
U = 8
NB0 = 2 * TOK // P + E0N
E1N, F1, CAP = 8, 512, 256
UP1 = 2 * CAP
REG1 = 3 * CAP
ROW = D + 1
SKIP = 1 << 20


class Named:
    pass


def tensors(nc, ctx):
    m = Named()

    def sb(name, shape, dt=F32):
        return ctx.enter_context(nc.sbuf_tensor(name, shape, dt))

    m.ident = sb("ident", [P, P])
    m.identb = sb("identb", [P, P], BF16)
    m.upper = sb("upper", [P, P], BF16)
    m.upperf = sb("upperf", [P, P])
    m.onesb = sb("onesb", [P, P], BF16)
    m.sel = sb("sel", [80, NC, P], BF16)
    m.hmask = sb("hmask", [KR, 2])
    m.iota_e = sb("iota_e", [P, E0N])
    m.ids = sb("ids", [P, NT, 2], I32)
    m.side = sb("side", [P, 3, QT, 2])
    m.padrow = sb("padrow", [P, 2 * ROW])
    m.number = sb("number", [P, 1])
    m.wq, m.wk, m.wv = ([sb(f"{w}{L}", [P, P]) for L in (0, 1)] for w in ("wq", "wk", "wv"))
    m.vb = [sb(f"vb{L}", [P, B, NC, 32]) for L in (0, 1)]
    m.kst = sb("kst", [KR, B, NC, 2, S2], BF16)
    m.wp = sb("wp", [P, P])
    m.bp = sb("bp", [P, P])
    m.bq = sb("bq", [P, 1])
    m.bk = sb("bk", [P, 1])
    m.bv = sb("bv", [P, P])
    m.wg0 = sb("wg0", [P, E0N])
    m.bg0 = sb("bg0", [P, 2, E0N])
    m.bgs = sb("bgs", [P, E0N])
    m.wg1 = sb("wg1", [P, E1N])
    m.w1_0 = sb("w1_0", [P, E0N * F0])
    m.w2_0 = sb("w2_0", [P, 2, E0N * D])
    m.b1_0 = sb("b1_0", [P, E0N, 2])
    m.b2_0 = sb("b2_0", [P, E0N * D])
    m.b1_1 = sb("b1_1", [P, E1N, 4])
    m.x = sb("x", [P, NT, D])
    m.ctxr = sb("ctxr", [P, 4, P])
    m.ctxT = sb("ctxT", [P, 512])
    m.kh = sb("kh", [P, 512], BF16)
    m.km = sb("km", [P, 512], BF16)
    m.kl = sb("kl", [P, 512], BF16)
    m.krep = sb("krep", [KR, NC, B, S2], BF16)
    m.mi = sb("mi", [P, 2, S2], I32)
    m.mf = sb("mf", [P, 2, S2])
    m.pi = sb("pi", [S2, B], I32)
    m.pf = sb("pf", [S2, B])
    m.keep = sb("keep", [S2, B, S], BF16)
    m.subT = sb("subT", [S2, S])
    m.live = sb("live", [P, B, S], BF16)
    m.mb = sb("mb", [S2, B, S], BF16)
    m.st = sb("st", [P, 2, 2, QT, 6])
    m.mv = sb("mv", [P, 2, 2, QT, 2])
    m.ve = sb("ve", [P, 2, 2, QT])
    m.ln = sb("ln", [P, 2, 2, QT])
    m.g = sb("g", [P, 2, 2, QT])
    m.t = sb("t", [P, 2, 2, QT])
    m.u = sb("u", [P, 2, 2, QT])
    m.rs = sb("rs", [P, 2, 2, QT])
    m.xn = sb("xn", [P, 2, QT, D])
    m.xnT = sb("xnT", [P, 2, S])
    m.qf = sb("qf", [P, 2, S])
    m.qr = sb("qr", [P, 2, S])
    m.qh = sb("qh", [P, 2, S], BF16)
    m.qm = sb("qm", [P, 2, S], BF16)
    m.ql = sb("ql", [P, 2, S], BF16)
    m.qst = sb("qst", [KR, 3, NC, S], BF16)
    m.mx = sb("mx", [P, 2, QT, H], BF16)
    m.rm = sb("rm", [80, 2, S], BF16)
    m.pT = sb("pT", [P, NC, S])
    m.oT = sb("oT", [P, 2, 2, S])
    m.rec = sb("rec", [P, 2, 2 * NC, 2])
    m.att = sb("att", [P, 2, 2 * NC, 2, DH])
    m.attT = sb("attT", [P, 2, S])
    m.xl = sb("xl", [P, 2, 2, QT, ROW])
    m.xlT = sb("xlT", [P, 2, S])
    m.lg = sb("lg", [P, NT, E0N])
    m.v8 = sb("v8", [P, NT, 8])
    m.i8 = sb("i8", [P, NT, 8], U32)
    m.oh = sb("oh", [P, 2, QT, 2, E0N], BF16)
    m.s1 = sb("s1", [P, 2, 2, E0N], BF16)
    m.s2 = sb("s2", [P, 3, 2, E0N], BF16)
    m.rt = sb("rt", [P, 2, QT, 2, E0N])
    m.rk = sb("rk", [P, 2, QT, 2])
    m.rb = sb("rb", [P, 2, QT, 2])
    m.ro = sb("ro", [P, 2, QT, 2])
    m.slf = sb("slf", [P, 2, QT, 2])
    m.slot = sb("slot", [P, NT, 2], U32)
    m.wt = sb("wt", [P, 2, NT])
    m.wa = sb("wa", [P, NT, E1N])
    m.wb = sb("wb", [P, NT])
    m.wc = sb("wc", [P, NT])
    m.wd = sb("wd", [P, NT])
    m.we = sb("we", [P, NT])
    m.cnt = sb("cnt", [P, 2, E0N])
    m.tb = sb("tb", [P, 10, E0N])
    m.be = sb("be", [P, 2])
    m.br = sb("br", [P, 2])
    m.bs = sb("bs", [P, 2])
    m.tot = sb("tot", [P, E0N], I32)
    m.toi = sb("toi", [P, E0N], I32)
    m.blk_e = sb("blk_e", [1, NB0], I32)
    m.blk_r = sb("blk_r", [1, NB0], I32)
    m.pad_r = sb("pad_r", [1, E0N], I32)
    m.xb = sb("xb", [P, 2 * E1N, ROW])
    m.xbT = sb("xbT", [P, 2, S])
    m.hb = sb("hb", [P, 2, F0])
    m.hT = sb("hT", [P, 2, 4 * S])
    m.yb = sb("yb", [P, 8, D])
    m.w1b = sb("w1b", [P, 2, F0])
    m.place = sb("place", [P, NB0], I32)
    m.ps = [ctx.enter_context(nc.psum_tensor(f"ps{i}", [P, 512], F32)) for i in range(8)]
    m.w1_1 = m.w1_0[:, :].rearrange("p (e f) -> p e f", e=E1N)
    m.w2_1 = m.w2_0[:, :, :].rearrange("p g (e d) -> p (g e d)", e=E0N).rearrange("p (e g d) -> p e g d", e=E1N, g=4)
    m.b2_1 = m.b2_0[:, 0:E1N * D]
    m.last = m.w1_0[:, :].rearrange("p (k t d) -> p k t d", k=2, d=D)
    m.yl = m.hT[:, 0, :].rearrange("p (n k t d) -> p n k t d", n=2, k=2, t=QT)
    m.zero = m.hT[:, 0, :]
    m.kf = m.xbT[:, :, :].rearrange("p n q -> p (n q)")
    m.kr = m.hb[:, :, :].rearrange("p n q -> p (n q)")
    m.self32 = m.pT[0:80, 0:4, :].rearrange("p c q -> p (c q)")
    m.ctxD = m.pT[:, 4:8, :].rearrange("p c q -> p (c q)").rearrange("p (b k) -> p b k", b=B)
    return m


def mixture_kernel(nc, a, out):
    with ExitStack() as ctx:
        m = tensors(nc, ctx)
        xs0 = nc.dram_tensor("xs0", [PAD0 + P, ROW], F32).ap()
        xs1 = nc.dram_tensor("xs1", [E1N * REG1, ROW], F32).ap()
        ys = [nc.dram_tensor(f"ys{L}", [2 * TOK, D], F32).ap() for L in (0, 1)]
        PA, PT_, PO, PM, PJ, PG = m.ps[0:2], m.ps[2:4], m.ps[4], m.ps[5], m.ps[6], m.ps[7]
        sem = Named()
        sem.in_q = ctx.enter_context(nc.semaphore("in_q"))
        sem.in_l1 = ctx.enter_context(nc.semaphore("in_l1"))
        sem.in_small = ctx.enter_context(nc.semaphore("in_small"))
        sem.zero_ok = ctx.enter_context(nc.semaphore("zero_ok"))
        sem.vb_ok = ctx.enter_context(nc.semaphore("vb_ok"))
        sem.sub_ok = ctx.enter_context(nc.semaphore("sub_ok"))
        sem.xp_ok = ctx.enter_context(nc.semaphore("xp_ok"))
        sem.v0_ok = ctx.enter_context(nc.semaphore("v0_ok"))
        sem.row_ok = ctx.enter_context(nc.semaphore("row_ok"))
        sem.row_ps = ctx.enter_context(nc.semaphore("row_ps"))
        sem.sel_ok = ctx.enter_context(nc.semaphore("sel_ok"))
        sem.ctxD_ok = ctx.enter_context(nc.semaphore("ctxD_ok"))
        sem.in_place = ctx.enter_context(nc.semaphore("in_place"))
        sem.in_const = ctx.enter_context(nc.semaphore("in_const"))
        sem.in_ctx = ctx.enter_context(nc.semaphore("in_ctx"))
        sem.in_mask = ctx.enter_context(nc.semaphore("in_mask"))
        sem.in_ffn = ctx.enter_context(nc.semaphore("in_ffn"))
        sem.in_w1 = ctx.enter_context(nc.semaphore("in_w1"))
        sem.filled = ctx.enter_context(nc.semaphore("filled"))
        sem.v_step = ctx.enter_context(nc.semaphore("v_step"))
        sem.a_step = ctx.enter_context(nc.semaphore("a_step"))
        sem.g_step = ctx.enter_context(nc.semaphore("g_step"))
        sem.ctx_ps = ctx.enter_context(nc.semaphore("ctx_ps"))
        sem.ctx_ok = ctx.enter_context(nc.semaphore("ctx_ok"))
        sem.k_ps = ctx.enter_context(nc.semaphore("k_ps"))
        sem.k_split = ctx.enter_context(nc.semaphore("k_split"))
        sem.krep_in = ctx.enter_context(nc.semaphore("krep_in"))
        sem.kst_ok = ctx.enter_context(nc.semaphore("kst_ok"))
        sem.v_ps = ctx.enter_context(nc.semaphore("v_ps"))
        sem.v_ok = ctx.enter_context(nc.semaphore("v_ok"))
        sem.sub_ps = ctx.enter_context(nc.semaphore("sub_ps"))
        sem.keep_ok = ctx.enter_context(nc.semaphore("keep_ok"))
        sem.live_ps = ctx.enter_context(nc.semaphore("live_ps"))
        sem.live_ok = ctx.enter_context(nc.semaphore("live_ok"))
        sem.var1 = ctx.enter_context(nc.semaphore("var1"))
        sem.guess1 = ctx.enter_context(nc.semaphore("guess1"))
        sem.xn_ok = ctx.enter_context(nc.semaphore("xn_ok"))
        sem.xn_ps = ctx.enter_context(nc.semaphore("xn_ps"))
        sem.xnT_ok = ctx.enter_context(nc.semaphore("xnT_ok"))
        sem.q_ps = ctx.enter_context(nc.semaphore("q_ps"))
        sem.qf_ok = ctx.enter_context(nc.semaphore("qf_ok"))
        sem.qh_ok = ctx.enter_context(nc.semaphore("qh_ok"))
        sem.qr_ok = ctx.enter_context(nc.semaphore("qr_ok"))
        sem.qm_ok = ctx.enter_context(nc.semaphore("qm_ok"))
        sem.ql_ok = ctx.enter_context(nc.semaphore("ql_ok"))
        sem.a_ps = ctx.enter_context(nc.semaphore("a_ps"))
        sem.mx_ok = ctx.enter_context(nc.semaphore("mx_ok"))
        sem.mx_ps = ctx.enter_context(nc.semaphore("mx_ps"))
        sem.rm_ok = ctx.enter_context(nc.semaphore("rm_ok"))
        sem.t_ps = ctx.enter_context(nc.semaphore("t_ps"))
        sem.pT_ok = ctx.enter_context(nc.semaphore("pT_ok"))
        sem.o_ps = ctx.enter_context(nc.semaphore("o_ps"))
        sem.oT_ok = ctx.enter_context(nc.semaphore("oT_ok"))
        sem.on_ps = ctx.enter_context(nc.semaphore("on_ps"))
        sem.att_ok = ctx.enter_context(nc.semaphore("att_ok"))
        sem.at_ps = ctx.enter_context(nc.semaphore("at_ps"))
        sem.attT_ok = ctx.enter_context(nc.semaphore("attT_ok"))
        sem.pj_ps = ctx.enter_context(nc.semaphore("pj_ps"))
        sem.x1_ok = ctx.enter_context(nc.semaphore("x1_ok"))
        sem.var2 = ctx.enter_context(nc.semaphore("var2"))
        sem.guess2 = ctx.enter_context(nc.semaphore("guess2"))
        sem.xl_ok = ctx.enter_context(nc.semaphore("xl_ok"))
        sem.xl2_ok = ctx.enter_context(nc.semaphore("xl2_ok"))
        sem.xl_ps = ctx.enter_context(nc.semaphore("xl_ps"))
        sem.xlT_ok = ctx.enter_context(nc.semaphore("xlT_ok"))
        sem.lg_ps = ctx.enter_context(nc.semaphore("lg_ps"))
        sem.lg_ok = ctx.enter_context(nc.semaphore("lg_ok"))
        sem.oh_ok = ctx.enter_context(nc.semaphore("oh_ok"))
        sem.rank_ps = ctx.enter_context(nc.semaphore("rank_ps"))
        sem.slot_ok = ctx.enter_context(nc.semaphore("slot_ok"))
        sem.cnt_ps = ctx.enter_context(nc.semaphore("cnt_ps"))
        sem.gate_d = ctx.enter_context(nc.semaphore("gate_d"))
        sem.gate_e = ctx.enter_context(nc.semaphore("gate_e"))
        sem.gate_ok = ctx.enter_context(nc.semaphore("gate_ok"))
        sem.table_ok = ctx.enter_context(nc.semaphore("table_ok"))
        sem.pad_ok = ctx.enter_context(nc.semaphore("pad_ok"))
        sem.padded = ctx.enter_context(nc.semaphore("padded"))
        sem.mbc_ok = ctx.enter_context(nc.semaphore("mbc_ok"))
        sem.bx_ps = ctx.enter_context(nc.semaphore("bx_ps"))
        sem.bxT_ok = ctx.enter_context(nc.semaphore("bxT_ok"))
        sem.place_ok = ctx.enter_context(nc.semaphore("place_ok"))
        sem.bh_ps = ctx.enter_context(nc.semaphore("bh_ps"))
        sem.bw_ok = ctx.enter_context(nc.semaphore("bw_ok"))
        sem.bh_ok = ctx.enter_context(nc.semaphore("bh_ok"))
        sem.by_ps = ctx.enter_context(nc.semaphore("by_ps"))
        sem.by_ok = ctx.enter_context(nc.semaphore("by_ok"))
        sem.ex_ps = ctx.enter_context(nc.semaphore("ex_ps"))
        sem.exT_ok = ctx.enter_context(nc.semaphore("exT_ok"))
        sem.eh_ps = ctx.enter_context(nc.semaphore("eh_ps"))
        sem.ehT_ok = ctx.enter_context(nc.semaphore("ehT_ok"))
        sem.ey_ps = ctx.enter_context(nc.semaphore("ey_ps"))
        sem.ey_ok = ctx.enter_context(nc.semaphore("ey_ok"))
        sem.eb_in = ctx.enter_context(nc.semaphore("eb_in"))
        sem.xo_ok = ctx.enter_context(nc.semaphore("xo_ok"))
        sem.stored = ctx.enter_context(nc.semaphore("stored"))

        def sems(name, n):
            return [ctx.enter_context(nc.semaphore(f"{name}{i}")) for i in range(n)]

        in_x, window_in, last_in = sems("in_x", 4), sems("window_in", E1N), sems("last_in", 4)
        qst_in, yl_in, xb_in = sems("qst_in", 3), sems("yl_in", 2), sems("xb_in", U)
        sent = [sems("sent_a", 2), sems("sent_b", 2)]
        back = [sems("back_a", U), sems("back_b", 4)]
        wq, wk, wv, vb = m.wq, m.wk, m.wv, m.vb
        EN = [E0N, E1N]
        block = ctx.enter_context(nc.Block())

        def wait(eng, which, value):
            if not isinstance(value, int) or value > 0:
                eng.wait_ge(which, value)

        def eight(engine, table, j, top):
            return nc.values_load_multi_w_load_instructions(
                table[0:1, j:j + 8], engines=[engine], min_val=0, max_val=top,
                skip_runtime_bounds_check_because="table() bounds them")[1]

        def pads(eng, engine, e):
            for r in eight(engine, m.pad_r, e, PAD0):
                eng.dma_start(xs0[bass.ds(r, P), :], m.padrow[:, 0:ROW]).then_inc(sem.padded, 16)

        def steps(L, order, first=-3, end=B + 2):
            for i in range(first, end):
                for stage, lead, *more in order:
                    if 0 <= i + lead < B:
                        stage(L, i + lead, *more)

        def store(sp, b):
            sp.wait_ge(sem.xo_ok, b + 1)
            sp.dma_start(out.rearrange("b s d -> (b s) d")[b * S:(b + 1) * S, :].rearrange("(t p) d -> p t d", p=P),
                         m.x[:, 2 * b:2 * b + 2, :]).then_inc(sem.stored, 16)

        @block.sync
        def _(sp):
            def load_x(g):
                sp.dma_start(m.x[:, 4 * g:4 * g + 4, :], a["x"].rearrange("b s d -> (b s) d")[2 * g * S:2 * (g + 1) * S, :]
                             .rearrange("(t p) d -> p t d", p=P)).then_inc(in_x[g], 16)

            for dst, src in ((m.ident[:], a["c_ident"]),
                             (m.ctxr[:], a["ctx_1024"].rearrange("b k d -> (b k) d").rearrange("(t p) d -> p t d", p=P)),
                             (wk[0][:], a["L0_xattn_Wk"])):
                sp.dma_start(dst, src).then_inc(sem.in_ctx, 16)
            load_x(0)
            sp.dma_start(wq[0][:], a["L0_xattn_Wq"]).then_inc(sem.in_q, 16)
            sp.dma_start(wv[0][:], a["L0_xattn_Wv"]).then_inc(sem.in_q, 16)

            def ffn_weights(L, b):
                E, EE = slice(2 * b, 2 * b + 2), 2 * b
                for dst, src in ((m.w1_0[:, EE * F0:(EE + 2) * F0].rearrange("p (e f) -> p e f", e=2), a["L0_ffn_W1"][E].rearrange("e d f -> d e f")),
                                 (m.w2_0[:, 0, EE * D:(EE + 2) * D].rearrange("p (e d) -> p e d", e=2), a["L0_ffn_W2"][E, 0:P, :].rearrange("e f d -> f e d")),
                                 (m.w2_0[:, 1, EE * D:(EE + 2) * D].rearrange("p (e d) -> p e d", e=2), a["L0_ffn_W2"][E, P:2 * P, :].rearrange("e f d -> f e d")),
                                 (m.b2_0[:, EE * D:(EE + 2) * D], a["L0_ffn_b2"][E].rearrange("e d -> (e d)").partition_broadcast(P))):
                    sp.dma_start(dst, src).then_inc(sem.in_ffn, 16)

            def fill(L, b):
                if b == 0:
                    sp.wait_ge(sem.in_place, 16 * 5)
                    sp.wait_ge(sem.zero_ok, 1)
                    sp.dma_start(xs0[PAD0:PAD0 + P, :], m.padrow[:, 0:ROW]).then_inc(sem.filled, 16)
                sp.dma_start(xs1[b * REG1 + CAP:b * REG1 + 2 * CAP, :].rearrange("(p r) d -> p (r d)", r=2),
                             m.padrow[:]).then_inc(sem.filled, 16)
                if b % 2:
                    i = b // 2
                    sp.dma_start(ys[1][i * 1024:(i + 1) * 1024, :].rearrange("(p r) d -> p (r d)", r=8),
                                 m.zero).then_inc(sem.filled, 16)

            def k_rows(L):
                for i, part in enumerate(K_PART):
                    sp.wait_ge(sem.k_split, 3 * L + part + 1)
                    if i == 0 and L == 1:
                        sp.wait_ge(sem.kst_ok, 1)
                    sp.dma_start(m.krep[16 * i:16 * i + 16, :, :, :].rearrange("r c b k -> r c (b k)"),
                                 [m.kh, m.km, m.kl][part][:, :]).then_inc(sem.krep_in, 16)

            k_rows(0)
            load_x(1)
            for dst, src in ((m.ids[:], a["c_ids"]), (m.side[:], a["c_side"]), (m.padrow[:], a["c_pad"]),
                             (m.iota_e[:], a["c_iota"]), (m.number[:], a["c_number"])):
                sp.dma_start(dst, src).then_inc(sem.in_place, 16)

            def q_rows(L, b):
                n = B * L + b
                src, ready = [m.qh, m.qm, m.ql], [sem.qh_ok, sem.qm_ok, sem.ql_ok]
                if n >= 3:
                    sp.wait_ge(sem.t_ps, 4 * (n - 2))
                for i, part in enumerate(Q_PART):
                    sp.wait_ge(ready[part], n + 1)
                    sp.dma_start(m.qst[16 * i:16 * i + 16, n % 3, :, :], src[part][:, n % 2, :]).then_inc(qst_in[n % 3], 16)

            def back_rows(L, b):
                n = B * L + b
                if b == 0:
                    for done in back[0]:
                        sp.wait_ge(done, 16 * NB0 // U)
                if n >= 2:
                    sp.wait_ge(sem.mbc_ok, n - 1)
                for k in range(2):
                    sp.dma_start(m.yl[:, n % 2, k, :, :],
                                 ys[L][k * TOK + b * S:k * TOK + (b + 1) * S, :].rearrange("(t p) d -> p t d", p=P)
                                 ).then_inc(yl_in[n % 2], 16)

            steps(0, [(q_rows, 2)], end=-1)
            for dst, src in ((wk[1][:], a["L1_xattn_Wk"]), (wv[1][:], a["L1_xattn_Wv"]), (m.bk[:], a["L1_xattn_bk"]),
                             (m.bv[:], a["L1_xattn_bv"].partition_broadcast(P)), (m.bq[:], a["L1_xattn_bq"]), (wq[1][:], a["L1_xattn_Wq"])):
                sp.dma_start(dst, src).then_inc(sem.in_l1, 16)
            for dst, src in ((m.bp[:], a["L0_xattn_bp"].partition_broadcast(P)), (m.wp[:], a["L0_xattn_Wp"]),
                             (m.wg0[:], a["L0_ffn_Wg"]), (m.bg0[:, 0, :], a["L0_ffn_bg"].partition_broadcast(P)),
                             (m.bg0[:, 1, :], a["L0_ffn_bias"].partition_broadcast(P)), (m.wg1[:], a["L1_ffn_Wg"]),
                             (m.b1_1[:], a["c_b1T"]), (m.b1_0[:], a["c_b1T0"])):
                sp.dma_start(dst, src).then_inc(sem.in_small, 16)
            load_x(2)
            steps(0, [(q_rows, 2)], first=-1, end=0)
            k_rows(1)
            load_x(3)
            steps(0, [(q_rows, 2), (ffn_weights, 0), (fill, 0)], first=0)
            sp.wait_ge(sem.pad_ok, 1)
            pads(sp, mybir.EngineType.SP, 0)
            sp.wait_ge(sem.table_ok, 1)
            for done in sent[0]:
                sp.wait_ge(done, 16 * NT)
            sp.wait_ge(sem.padded, 16 * E0N)
            sp.wait_ge(sem.filled, 16 * (1 + E1N + 4))

            def load_block(j, u, wait):
                if u == 0:
                    row[:] = eight(mybir.EngineType.SP, m.blk_r, j, PAD0)
                r = row[u]
                if wait is not None:
                    sp.wait_ge(sem.place_ok, wait)
                sp.dma_start(m.xb[:, u, :], xs0[bass.ds(r, P), :]).then_inc(xb_in[u], 16)

            row = []
            for j in range(NB0):
                load_block(j, j % U, j - U + 1 if j >= U else None)

            sp.wait_ge(sem.by_ok, NB0)

            def first_results(L, b):
                back_rows(0, b)

            def expert_weights(L, e):
                sp.dma_start(m.w1_1[:, e, :], a["L1_ffn_W1"][e]).then_inc(sem.in_w1, 16)
                sp.dma_start(m.w2_1[:, e, :, :], a["L1_ffn_W2"][e].rearrange("(c p) d -> p c d", p=P)).then_inc(sem.in_w1, 16)
                if e == 0:
                    sp.dma_start(m.b2_1, a["L1_ffn_b2"].rearrange("e d -> (e d)").partition_broadcast(P)).then_inc(sem.in_w1, 16)

            steps(1, [(first_results, 3), (q_rows, 2), (expert_weights, 0)])
            sp.wait_ge(sem.table_ok, 2)
            for done in sent[1]:
                sp.wait_ge(done, 16 * NT)
            row = eight(mybir.EngineType.SP, m.blk_r, 0, E1N * REG1 - CAP)
            for e in range(E1N):
                for h in range(2):
                    sp.dma_start(m.xb[:, 2 * e + h, :], xs1[bass.ds(row[e] + h * P, P), :]).then_inc(window_in[e], 16)
            for done in back[1]:
                sp.wait_ge(done, 16 * 2 * E1N // len(back[1]))
            for g in range(B // 2):
                for k in range(2):
                    sp.dma_start(m.last[:, k, 4 * g:4 * g + 4, :],
                                 ys[1][k * TOK + 2 * g * S:k * TOK + 2 * (g + 1) * S, :].rearrange("(t p) d -> p t d", p=P)
                                 ).then_inc(last_in[g], 16)
            for b in range(B - 1):
                store(sp, b)
            store(sp, B - 1)
            sp.wait_ge(sem.stored, 16 * B)

        @block.tensor
        def _(pe):
            mm = pe.matmul
            pe.wait_ge(sem.in_ctx, 16 * 3)
            for t in range(4):
                i = pe.transpose(PA[0][:, t * P:(t + 1) * P], m.ctxr[:, t, :], m.ident[:])
            i.then_inc(sem.ctx_ps, 1)
            pe.wait_ge(sem.ctx_ok, 1)
            mm(PA[1][:, :], wk[0][:], m.ctxT[:]).then_inc(sem.k_ps, 1)
            pe.wait_ge(sem.in_q, 32)
            pe.wait_ge(sem.ctxD_ok, 1)
            for g in range(2):
                for b in range(4):
                    i = mm(PT_[g][:, b * P:(b + 1) * P], m.ctxD[:, 4 * g + b, :], wv[0][:])
                i.then_inc(sem.v_ps, 1)
            pe.wait_ge(sem.keep_ok, 1)
            for t in range(2):
                i = pe.transpose(PG[0:S2, t * P:(t + 1) * P], m.mf[:, t, :], m.ident[:])
            i.then_inc(sem.sub_ps, 1)

            def second_keys():
                pe.wait_ge(sem.in_l1, 16 * 6)
                pe.wait_ge(sem.v_ok, 2)
                mm(PT_[0][:, :], wk[1][:], m.ctxT[:]).then_inc(sem.k_ps, 1)
                for g in range(2):
                    for b in range(4):
                        i = mm([PT_[1], PO][g][:, b * P:(b + 1) * P], m.ctxD[:, 4 * g + b, :], wv[1][:])
                    i.then_inc(sem.v_ps, 1)

            def live_keys():
                pe.wait_ge(sem.keep_ok, 2)
                for g in range(4):
                    mm([PA[0], PA[1], PT_[0], PT_[1]][g][:], m.onesb[0:S2, :], m.keep[:, 2 * g:2 * g + 2, :]).then_inc(sem.live_ps, 1)

            def block_rows():
                pe.wait_ge(sem.row_ok, 1)
                mm(PG[0:1, 0:NB0], m.be[0:NB0, 0:1], m.ident[0:NB0, 0:NB0])
                mm(PG[0:1, NB0:2 * NB0], m.br[0:NB0, 1:2], m.ident[0:NB0, 0:NB0]).then_inc(sem.row_ps, 1)

            read = {"PM": None, "PJ": None, "PG": (sem.sub_ok, 1)}

            def after_read(bank):
                if read[bank]:
                    pe.wait_ge(read[bank][0], read[bank][1])

            def xn_transpose(L, b):
                n = B * L + b
                pe.wait_ge(sem.xn_ok, n + 1)
                after_read("PM")
                read["PM"] = (sem.xnT_ok, n + 1)
                for t in range(QT):
                    i = pe.transpose(PM[:, t * P:(t + 1) * P], m.xn[:, n % 2, t, :], m.ident[:])
                i.then_inc(sem.xn_ps, 1)

            def q_product(L, b):
                n = B * L + b
                if n == 0:
                    pe.wait_ge(sem.in_q, 32)
                pe.wait_ge(sem.xnT_ok, n + 1)
                after_read("PJ")
                read["PJ"] = (sem.qr_ok, n + 1)
                mm(PJ[:, 0:S], wq[L][:], m.xnT[:, n % 2, :]).then_inc(sem.q_ps, 1)

            def scores(L, b, u):
                n, t, g = B * L + b, u // 2, u % 2
                if u == 0:
                    pe.wait_ge(sem.kst_ok, L + 1)
                    pe.wait_ge(qst_in[n % 3], 16 * NP * (n // 3 + 1))
                if 4 * n + u >= 2:
                    pe.wait_ge(sem.mx_ok, 4 * n + u - 1)
                o = PA[u % 2]
                if L == 1:
                    mm(o[:, :], m.mb[:, b, t * P:(t + 1) * P], m.sel[0:S2, 0:4, :], start=True, stop=False,
                       skip_group_check=True)
                for c in range(4):
                    i = mm(o[:, c * P:(c + 1) * P], m.qst[:, n % 3, 4 * g + c, t * P:(t + 1) * P],
                           m.kst[:, b, 4 * g + c, :, :], start=(L == 0), stop=True, skip_group_check=True)
                i.then_inc(sem.a_ps, 1)

            def max_transpose(L, b):
                n = B * L + b
                pe.wait_ge(sem.mx_ok, 4 * n + 4)
                pe.wait_ge(sem.sel_ok, 1)
                after_read("PG")
                read["PG"] = (sem.rm_ok, n + 1)
                for t in range(QT):
                    i = pe.transpose(PG[:, :].bitcast(BF16)[64:64 + H, S + t * P:S + (t + 1) * P], m.mx[:, n % 2, t, :], m.identb[:])
                i.then_inc(sem.mx_ps, 1)

            def scores_T(L, b, u):
                n = B * L + b
                if u == 0:
                    pe.wait_ge(sem.rm_ok, n + 1)
                if n == 0 and u < 2:
                    if u == 0:
                        pe.wait_ge(sem.k_split, 4)
                    else:
                        pe.wait_ge(sem.v_ok, 3)
                if 4 * n + u >= 2:
                    pe.wait_ge(sem.pT_ok, 4 * n + u - 1)
                for c in range(2):
                    o = PT_[u % 2][:, c * S:(c + 1) * S]
                    mm(o, m.sel[:, 2 * u + c, :], m.rm[:, n % 2, :], start=(c == 0), stop=False, skip_group_check=True)
                    i = mm(o, m.kst[:, b, 2 * u + c, :, :], m.qst[:, n % 3, 2 * u + c, :], start=False, stop=True,
                           skip_group_check=True)
                i.then_inc(sem.t_ps, 1)

            def values(L, b):
                n = B * L + b
                if n == 0:
                    pe.wait_ge(sem.v_ok, 4)
                pe.wait_ge(sem.pT_ok, 4 * n + 4)
                if n >= 1:
                    pe.wait_ge(sem.att_ok, n)
                for c in range(NC):
                    r = 32 * (c % 4)
                    i = mm(PO[r:r + 32, (c // 4) * S:(c // 4 + 1) * S], vb[L][:, b, c, :], m.pT[:, c, :])
                i.then_inc(sem.o_ps, 1)

            def o_transpose(L, b):
                n = B * L + b
                pe.wait_ge(sem.oT_ok, n + 1)
                for t in range(QT):
                    for g in range(2):
                        i = pe.transpose(PO[:, (2 * t + g) * P:(2 * t + g + 1) * P], m.oT[:, n % 2, g, t * P:(t + 1) * P], m.ident[:])
                i.then_inc(sem.on_ps, 1)

            def att_transpose(L, b):
                pe.wait_ge(sem.att_ok, b + 1)
                after_read("PM")
                read["PM"] = (sem.attT_ok, b + 1)
                for t in range(QT):
                    i = pe.transpose(PM[:, t * P:(t + 1) * P], m.att[:, b % 2, 8 * t:8 * t + 8, :, :], m.ident[:])
                i.then_inc(sem.at_ps, 1)

            def project(L, b):
                pe.wait_ge(sem.in_small, 16 * 8)
                pe.wait_ge(sem.attT_ok, b + 1)
                after_read("PJ")
                read["PJ"] = (sem.x1_ok, b + 1)
                for t in range(QT):
                    i = mm(PJ[:, t * P:(t + 1) * P], m.attT[:, b % 2, t * P:(t + 1) * P], m.wp[:])
                i.then_inc(sem.pj_ps, 1)

            def xl_transpose(L, b):
                n = B * L + b
                pe.wait_ge(sem.xl_ok, n + 1)
                after_read("PM")
                read["PM"] = (sem.xlT_ok, n + 1)
                for t in range(QT):
                    i = pe.transpose(PM[:, t * P:(t + 1) * P], m.xl[:, n % 2, 0, t, 0:D], m.ident[:])
                i.then_inc(sem.xl_ps, 1)

            def router(L, b):
                n = B * L + b
                pe.wait_ge(sem.xlT_ok, n + 1)
                after_read("PG")
                read["PG"] = (sem.oh_ok, n + 1)
                for t in range(QT):
                    o = PG[:, t * EN[L]:(t + 1) * EN[L]]
                    i = mm(o, m.xlT[:, n % 2, t * P:(t + 1) * P], [m.wg0, m.wg1][L][:])
                i.then_inc(sem.lg_ps, 1)

            def ranks(L, b):
                n, w = B * L + b, 2 * EN[L]
                pe.wait_ge(sem.oh_ok, n + 1)
                after_read("PG")
                read["PG"] = (sem.slot_ok, n + 1)
                o = [PG[:, 64 + t * w:64 + (t + 1) * w] for t in range(QT)]
                oh = [m.oh[:, n % 2, t, :, 0:EN[L]] for t in range(QT)]
                mm(o[0], m.upper[:], oh[0], start=True, stop=False, skip_group_check=True)
                mm(o[0], m.onesb[:], m.s2[:, (b + 2) % 3, :, 0:EN[L]], start=False, stop=True, skip_group_check=True)
                mm(o[1], m.upper[:], oh[1], start=False, stop=False, skip_group_check=True)
                mm(o[1], m.onesb[:], m.s1[:, n % 2, :, 0:EN[L]], start=False, stop=True, skip_group_check=True).then_inc(sem.rank_ps, 1)

            def counts(L):
                pe.wait_ge(sem.slot_ok, B * (L + 1))
                mm(PG[:, 0:2 * EN[L]], m.onesb[:], m.s2[:, (B - 1) % 3, :, 0:EN[L]]).then_inc(sem.cnt_ps, 1)

            def order(L):
                o = [(xn_transpose, 2), (scores_T, 0, 0), (scores_T, 0, 1), (q_product, 2)]
                if L == 0:
                    o += [(att_transpose, -1), (scores, 1, 0), (ranks, -2), (scores_T, 0, 2), (project, -1)]
                else:
                    o += [(scores, 1, 0), (ranks, -2), (scores_T, 0, 2)]
                return o + [(scores, 1, 1), (scores_T, 0, 3), (scores, 1, 2), (scores, 1, 3), (values, 0),
                            (xl_transpose, -1), (max_transpose, 1), (o_transpose, 0), (router, -1)]

            steps(0, order(0), end=0)
            second_keys()
            steps(0, order(0), first=0)
            counts(0)
            live_keys()
            block_rows()
            pe.wait_ge(sem.live_ok, 4)

            def block_step(s, u, first=0, last=2):
                if first <= 0:
                    wait(pe, sem.bxT_ok, s - 1)
                    pe.wait_ge(xb_in[u], (s - u) * (16 // U) + 16)
                    pe.transpose(m.ps[u % 2][:, 0:P], m.xb[:, u, 0:D], m.ident[:]).then_inc(sem.bx_ps, 1)
                if first <= 1 <= last:
                    pe.wait_ge(sem.bxT_ok, s)
                    pe.wait_ge(sem.bw_ok, s)
                    wait(pe, sem.bh_ok, s - 2)
                    for g in range(2):
                        i = pe.matmul(m.ps[2 + (u - 1) % 2][:, g * P:(g + 1) * P], m.w1b[:, (u - 1) % 2, g * P:(g + 1) * P],
                                      m.xbT[:, (u - 1) % 2, 0:P])
                    i.then_inc(sem.bh_ps, 1)
                if first <= 2 <= last:
                    if (s - 2) % 8 == 0:
                        expert.extend(eight(mybir.EngineType.PE, m.blk_e, s - 2, E0N - 1))
                    e = expert[s - 2]
                    pe.wait_ge(sem.bh_ok, s - 1)
                    wait(pe, sem.by_ok, s - 3)
                    for g in range(2):
                        i = pe.matmul(m.ps[6 + (u - 2) % 2][:, 0:D], m.hT[:, (u - 2) % 2, g * P:(g + 1) * P],
                                      m.w2_0[:, g, bass.ds(e * D, D)], start=(g == 0), stop=(g == 1))
                    i.then_inc(sem.by_ps, 1)

            pe.wait_ge(sem.table_ok, 1)
            pe.wait_ge(sem.in_ffn, 16 * 4 * B)
            expert = []
            for s in range(NB0 + 2):
                block_step(s, s % U, first=max(0, s - NB0 + 1), last=s)
            pe.wait_ge(sem.by_ok, NB0)

            steps(1, order(1))
            counts(1)

            def expert_x(e):
                pe.wait_ge(window_in[e], 32)
                if e >= 1:
                    pe.wait_ge(sem.exT_ok, e)
                for t in range(2):
                    i = pe.transpose(PM[:, t * P:(t + 1) * P], m.xb[:, 2 * e + t, 0:D], m.ident[:])
                i.then_inc(sem.ex_ps, 1)

            def expert_h(e):
                pe.wait_ge(sem.exT_ok, e + 1)
                for g in range(4):
                    if 4 * e + g >= 4:
                        pe.wait_ge(sem.ehT_ok, 4 * e + g - 3)
                    mm(m.ps[g][:, 0:S], m.w1_1[:, e, g * P:(g + 1) * P], m.xbT[:, e % 2, :]).then_inc(sem.eh_ps, 1)

            def expert_y(e):
                if e >= 2:
                    pe.wait_ge(sem.ey_ok, e - 1)
                o = [PJ, PG][e % 2]
                pe.wait_ge(sem.ehT_ok, 4 * e + 4)
                for t in range(2):
                    for g in range(4):
                        i = mm(o[:, t * P:(t + 1) * P], m.hT[:, e % 2, g * S + t * P:g * S + (t + 1) * P], m.w2_1[:, e, g, :],
                               start=(g == 0), stop=(g == 3))
                i.then_inc(sem.ey_ps, 1)

            pe.wait_ge(sem.table_ok, 2)
            pe.wait_ge(sem.in_w1, 16 * (2 * E1N + 1))
            expert_x(0)
            for e in range(E1N + 1):
                if e < E1N:
                    expert_h(e)
                if e + 1 < E1N:
                    expert_x(e + 1)
                if e >= 1:
                    expert_y(e - 1)

        @block.vector
        def _(dve):
            done = [0]

            def then(i):
                done[0] += 1
                i.then_inc(sem.v_step, 1)
                dve.wait_ge(sem.v_step, done[0])

            tt, ts, stt, copy = dve.tensor_tensor, dve.tensor_scalar, dve.scalar_tensor_tensor, dve.tensor_copy
            dve.memset(m.onesb[:], 1.0)
            dve.memset(m.rm[:], 0.0)
            dve.memset(m.s2[:], 0.0)
            dve.wait_ge(sem.ctx_ps, 1)
            copy(m.ctxT[:], PA[0][:]).then_inc(sem.ctx_ok, 1)

            def keys(L):
                dve.wait_ge(sem.krep_in, 16 * NP * (L + 1))
                if L == 1:
                    dve.wait_ge(sem.t_ps, 4 * B)
                for h in range(2):
                    i = ts(m.kst[:, :, :, h, :], m.krep[:].rearrange("r c b k -> r b c k"), m.hmask[:, h:h + 1], None, ALU.mult)
                i.then_inc(sem.kst_ok, 1)

            def split_keys(L):
                if L == 1:
                    dve.wait_ge(sem.in_l1, 16 * 6)
                    dve.wait_ge(sem.krep_in, 16 * NP)
                dve.wait_ge(sem.k_ps, L + 1)
                then(ts(m.kf[:], [PA[1], PT_[0]][L][:], m.bk[:, 0:1] if L else 0.0, None, ALU.add))
                copy(m.kh[:], m.kf[:]).then_inc(sem.k_split, 1)
                dve.wait_ge(sem.k_split, 3 * L + 1)
                then(tt(m.kr[:], m.kf[:], m.kh[:], ALU.subtract))
                copy(m.km[:], m.kr[:]).then_inc(sem.k_split, 1)
                dve.wait_ge(sem.k_split, 3 * L + 2)
                tt(m.kl[:], m.kr[:], m.km[:], ALU.subtract).then_inc(sem.k_split, 1)

            def split_values(L):
                if L == 1:
                    dve.wait_ge(sem.in_l1, 16 * 6)
                for g in range(2):
                    dve.wait_ge(sem.v_ps, 2 * L + g + 1)
                    for h in range(2):
                        rows = slice(64 * h, 64 * h + 64)
                        src = [PT_[0], PT_[1], PT_[1], PO][2 * L + g][rows, :].rearrange("p (b c h d) -> p b c h d", b=4, c=NC, h=2)[:, :, :, h, :]
                        dst = vb[L][rows, 4 * g:4 * g + 4, :, 8 * h:8 * h + 8]
                        if L == 0:
                            i = copy(dst, src)
                        else:
                            bv = m.bv[rows, :].rearrange("p (c h d) -> p c h d", c=NC, h=2)[:, :, h, :]
                            i = tt(dst, src, bv.unsqueeze(1).broadcast_to([64, 4, NC, DH]), ALU.add)
                    i.then_inc(sem.v_ok, 1)

            def live_queries():
                for g in range(4):
                    dve.wait_ge(sem.live_ps, g + 1)
                    ts(m.live[:, 2 * g:2 * g + 2, :], [PA[0], PA[1], PT_[0], PT_[1]][g][:].rearrange("p (b q) -> p b q", b=2), 1.0, None,
                       ALU.min).then_inc(sem.live_ok, 1)

            def statistics(v, n, b, ready):
                st, mv, ve = m.st[:, v], m.mv[:, v], m.ve[:, v]
                for t in range(QT):
                    i = dve.bn_stats(st[:, n % 2, t, :], m.x[:, 2 * b + t, :])
                then(i)
                for t in range(QT):
                    i = dve.bn_aggr(mv[:, n % 2, t, :], st[:, n % 2, t, :])
                then(i)
                ts(ve[:, n % 2, :], mv[:, n % 2, :, 1], EPS, None, ALU.add).then_inc(ready, 1)

            def root(v, n, guess):
                ve, g, u, r = (x[:, v, n % 2, :] for x in (m.ve, m.g, m.u, m.rs))
                dve.wait_ge(guess, n + 1)
                then(tt(u, g, g, ALU.mult))
                tv = m.t[:, v, n % 2, :]
                then(stt(tv, u, -0.5, ve, ALU.mult, ALU.mult))
                then(stt(r, tv, 1.5, g, ALU.add, ALU.mult))

            def combine(L, b):
                n = B * L + b
                if L == 0:
                    dve.wait_ge(yl_in[n % 2], 32 * (n // 2 + 1))
                else:
                    dve.wait_ge(last_in[b // 2], 32)
                for k in range(2):
                    for t in range(QT):
                        x = m.x[:, 2 * b + t, :]
                        i = stt(x, m.yl[:, n % 2, k, t, :] if L == 0 else m.last[:, k, 2 * b + t, :], m.wt[:, k, 2 * b + t:2 * b + t + 1], x, ALU.mult, ALU.add)
                    if k == 0:
                        then(i)
                if L == 1:
                    i.then_inc(sem.xo_ok, 1)
                    return
                i.then_inc(sem.mbc_ok, 1)
                dve.wait_ge(sem.mbc_ok, n + 1)

            def statistics1(L, b):
                if L == 0:
                    dve.wait_ge(in_x[b // 2], 16)
                if L == 1:
                    combine(0, b)
                statistics(0, B * L + b, b, sem.var1)

            def normal1(L, b):
                n = B * L + b
                root(0, n, sem.guess1)
                wait(dve, sem.xn_ps, n - 1)
                for t in range(QT):
                    i = ts(m.xn[:, n % 2, t, :], m.x[:, 2 * b + t, :], m.mv[:, 0, n % 2, t, 0:1], m.rs[:, 0, n % 2, t:t + 1],
                           ALU.subtract, ALU.mult)
                i.then_inc(sem.xn_ok, 1)

            def q_biased(L, b):
                n = B * L + b
                dve.wait_ge(sem.q_ps, n + 1)
                stt(m.qf[:, n % 2, :], PJ[:, 0:S], m.bq[:, 0:1], m.live[:, b, :], ALU.add, ALU.mult).then_inc(sem.qf_ok, 1)

            def q_rest(L, b):
                n = B * L + b
                dve.wait_ge(sem.qh_ok, n + 1)
                src = m.qf[:, n % 2, :] if L else PJ[:, 0:S]
                tt(m.qr[:, n % 2, :], src, m.qh[:, n % 2, :], ALU.subtract).then_inc(sem.qr_ok, 1)

            def q_low(L, b):
                n = B * L + b
                dve.wait_ge(sem.qm_ok, n + 1)
                if n >= 2:
                    dve.wait_ge(qst_in[(n - 2) % 3], 16 * NP * ((n - 2) // 3 + 1))
                tt(m.ql[:, n % 2, :], m.qr[:, n % 2, :], m.qm[:, n % 2, :], ALU.subtract).then_inc(sem.ql_ok, 1)

            def maximum(L, b, u):
                n = B * L + b
                dve.wait_ge(sem.a_ps, 4 * n + u + 1)
                if u == 0:
                    wait(dve, sem.mx_ps, n - 1)
                dve.tensor_reduce(m.mx[:, n % 2, u // 2, 8 * (u % 2):8 * (u % 2) + 8],
                                  PA[u % 2][:].rearrange("p (h k) -> p h k", h=8), AX.X, ALU.max).then_inc(sem.mx_ok, 1)

            def normalise(L, b):
                n = B * L + b
                dve.wait_ge(sem.on_ps, n + 1)
                o = PO[:].rearrange("p (g j) -> p g j", j=32)
                then(dve.reciprocal(m.rec[:, n % 2, :, :], o[:, :, 16:18]))
                if L == 0:
                    wait(dve, sem.at_ps, n - 1)
                tt(m.att[:, n % 2, :, :, :], o[:, :, 0:16].rearrange("p g (h d) -> p g h d", h=2),
                   m.rec[:, n % 2, :, :].unsqueeze(3).broadcast_to([P, 16, 2, DH]), ALU.mult).then_inc(sem.att_ok, 1)

            def residual(L, b):
                n = B * L + b
                x = m.x[:, 2 * b:2 * b + 2, :]
                if L == 0:
                    dve.wait_ge(sem.pj_ps, b + 1)
                    dve.wait_ge(sem.xp_ok, b + 1)
                    add = PJ[:, 0:S].rearrange("p (t d) -> p t d", t=QT)
                else:
                    dve.wait_ge(sem.att_ok, n + 1)
                    add = m.att[:, n % 2, :, :, :].rearrange("p (t c) h d -> p t (c h d)", t=QT)
                tt(x, x, add, ALU.add).then_inc(sem.x1_ok, 1)
                dve.wait_ge(sem.x1_ok, n + 1)
                statistics(1, n, b, sem.var2)

            def normal2(L, b):
                n = B * L + b
                root(1, n, sem.guess2)
                for e in range(2):
                    if e == n % 2:
                        wait(dve, sent[L][e], 64 * (b // 2))
                if L == 1 and b < 2:
                    dve.wait_ge(sent[0][b], 16 * NT)
                wait(dve, sem.xl_ps, n - 1)
                for t in range(QT):
                    i = ts(m.xl[:, n % 2, 0, t, 0:D], m.x[:, 2 * b + t, :], m.mv[:, 1, n % 2, t, 0:1], m.rs[:, 1, n % 2, t:t + 1],
                           ALU.subtract, ALU.mult)
                i.then_inc(sem.xl_ok, 1)

            def choose(L, b):
                n, E = B * L + b, EN[L]
                dve.wait_ge(sem.lg_ps, n + 1)
                lg, src = m.lg[:, 2 * b:2 * b + 2, 0:E], PG[:, 0:2 * E].rearrange("p (t e) -> p t e", t=QT)
                then(copy(lg, src) if L else tt(lg, src, m.bgs[:].unsqueeze(1).broadcast_to([P, QT, E]), ALU.add))
                for t in range(2 * b, 2 * b + 2):
                    i = dve.max(m.v8[:, t, :], m.lg[:, t, 0:E])
                then(i)
                for t in range(2 * b, 2 * b + 2):
                    i = dve.max_index(m.i8[:, t, :], m.v8[:, t, :], m.lg[:, t, 0:E])
                then(i)
                wait(dve, sem.rank_ps, n - 1)
                then(tt(m.oh[:, n % 2, :, :, 0:E], m.iota_e[:, 0:E].unsqueeze(1).unsqueeze(1).broadcast_to([P, QT, 2, E]),
                        m.i8[:, 2 * b:2 * b + 2, 0:2].unsqueeze(3).broadcast_to([P, QT, 2, E]), ALU.is_equal))
                then(tt(m.s1[:, n % 2, :, 0:E], m.s2[:, (b + 2) % 3, :, 0:E], m.oh[:, n % 2, 0, :, 0:E], ALU.add))
                tt(m.s2[:, b % 3, :, 0:E], m.s1[:, n % 2, :, 0:E], m.oh[:, n % 2, 1, :, 0:E], ALU.add).then_inc(sem.oh_ok, 1)

            def places(L, b):
                n, E = B * L + b, EN[L]
                dve.wait_ge(sem.rank_ps, n + 1)
                rank = PG[:, 64:64 + 4 * E].rearrange("p (t k e) -> p t k e", t=QT, k=2)
                rt, rk, rb, ro, slf = (x[:, n % 2] for x in (m.rt, m.rk, m.rb, m.ro, m.slf))
                then(tt(rt[:, :, :, 0:E], rank, m.oh[:, n % 2, :, :, 0:E], ALU.mult))
                then(dve.tensor_reduce(rk, rt[:, :, :, 0:E], AX.X, ALU.add))
                then(tt(rb, rk, m.side[:, 0, :, :], ALU.mult))
                if L == 1:
                    ts(ro, rk, float(CAP), float(SKIP), ALU.is_ge, ALU.mult)
                then(tt(rb, rb, m.side[:, 1 + L, :, :], ALU.add))
                dst = m.slot[:, 2 * b:2 * b + 2, :]
                idx = m.i8[:, 2 * b:2 * b + 2, 0:2]
                if L == 0:
                    stt(dst, idx, float(REG0), rb, ALU.mult, ALU.add).then_inc(sem.slot_ok, 1)
                else:
                    then(stt(slf, idx, float(REG1), rb, ALU.mult, ALU.add))
                    tt(dst, slf, ro, ALU.add).then_inc(sem.slot_ok, 1)

            def gates(L):
                v0, v1 = m.v8[:, :, 0], m.v8[:, :, 1]
                w0, w1 = m.wt[:, 0, :], m.wt[:, 1, :]
                if L == 1:
                    tt(m.wa[:], m.lg[:, :, 0:E1N], m.v8[:, :, 0:1].broadcast_to([P, NT, E1N]), ALU.subtract)
                tt(m.wd[:], v1, v0, ALU.subtract).then_inc(sem.gate_d, 1)
                dve.wait_ge(sem.gate_e, L + 1)
                if L == 0:
                    then(ts(m.wb[:], m.wc[:], 1.0, None, ALU.add))
                    then(dve.reciprocal(w0, m.wb[:]))
                    then(tt(w1, m.wc[:], w0, ALU.mult))
                else:
                    then(dve.tensor_reduce(m.wb[:], m.wa[:], AX.X, ALU.add))
                    then(dve.reciprocal(m.we[:], m.wb[:]))
                    then(tt(m.wc[:], m.wc[:], m.we[:], ALU.mult))
                    then(stt(m.wb[:], m.we[:], 1e-9, m.wc[:], ALU.add, ALU.add))
                    then(dve.reciprocal(m.wd[:], m.wb[:]))
                    tt(w0, m.we[:], m.wd[:], ALU.mult)
                    then(tt(w1, m.wc[:], m.wd[:], ALU.mult))

            def table(L):
                dve.wait_ge(sem.cnt_ps, L + 1)
                E = EN[L]
                R = slice(0, NB0)
                then(copy(m.cnt[R, :, 0:E], PG[R, 0:2 * E].rearrange("p (k e) -> p k e", k=2)))
                c0, c1, ie = m.cnt[R, 0, 0:E], m.cnt[R, 1, 0:E], m.iota_e[R, 0:E]
                r = [m.tb[R, i, 0:E] for i in range(10)]
                if L == 1:
                    then(ts(r[0][0:1], c0[0:1], float(CAP), float(CAP), ALU.min, ALU.add))
                    stt(m.blk_r[0:1, 0:E], ie[0:1], float(REG1), r[0][0:1], ALU.mult, ALU.add).then_inc(sem.table_ok, 1)
                    return
                then(ts(r[0], c0, float(UP0), None, ALU.add))
                stt(m.pad_r[0:1, :], ie[0:1], float(REG0), r[0][0:1], ALU.mult, ALU.add).then_inc(sem.pad_ok, 1)
                dve.memset(r[2], 1.0)
                then(stt(m.toi[R, :], c0, float(P - 1), c1, ALU.add, ALU.add))
                stt(r[5], ie, float(REG0), c1, ALU.mult, ALU.subtract)
                then(ts(m.tot[R, :], m.toi[R, :], 7, None, ALU.logical_shift_right))
                then(copy(r[1], m.tot[R, :]))
                then(dve.tensor_tensor_scan(r[3], r[2], r[1], 0.0, ALU.mult, ALU.add))
                ts(r[7], r[3], m.number[R, 0:1], None, ALU.is_le)
                then(tt(r[4], r[3], r[1], ALU.subtract))
                dve.tensor_reduce(m.be[R, 0:1], r[7], AX.X, ALU.add)
                then(stt(r[6], r[4], float(-P), r[5], ALU.mult, ALU.add))
                ts(m.br[R, 0:1], m.be[R, 0:1], float(E0N), 1e8, ALU.is_ge, ALU.mult)
                then(stt(r[8], ie, m.be[R, 0:1], r[6], ALU.is_equal, ALU.mult))
                then(dve.tensor_reduce(m.bs[R, 0:1], r[8], AX.X, ALU.add))
                then(stt(m.bs[R, 1:2], m.number[R, :], float(P), m.bs[R, 0:1], ALU.mult, ALU.add))
                stt(m.br[R, 1:2], m.bs[R, 1:2], float(UP0), m.br[R, 0:1], ALU.add, ALU.add).then_inc(sem.row_ok, 1)
                dve.wait_ge(sem.row_ps, 1)
                ts(m.blk_r[:, 0:NB0], PG[0:1, NB0:2 * NB0], float(PAD0), None, ALU.min)
                ts(m.blk_e[:, 0:NB0], PG[0:1, 0:NB0], float(E0N - 1), None, ALU.min).then_inc(sem.table_ok, 1)

            def order(L):
                return [(normalise, -1), (statistics1, 3), (choose, -2)] + ([(q_biased, 2)] if L == 1 else []) + [
                    (q_rest, 2), (maximum, 1, 0), (q_low, 2), (residual, -1), (maximum, 1, 1), (places, -2), (maximum, 1, 2),
                    (normal2, -1), (maximum, 1, 3), (normal1, 3)]

            dve.wait_ge(sem.in_mask, 32)
            ts(m.pf[:], m.pi[:], 0.0, None, ALU.not_equal)
            ts(m.mf[:], m.mi[:], 0.0, None, ALU.not_equal).then_inc(sem.keep_ok, 1)
            split_keys(0)
            steps(0, order(0), end=-1)
            dve.wait_ge(sem.vb_ok, 1)
            split_values(0)
            dve.wait_ge(sem.in_const, 16 * 3)
            keys(0)
            copy(m.identb[:], m.ident[:])
            copy(m.upper[:], m.upperf[:])
            copy(m.sel[:].rearrange("p c k -> p (c k)"), m.self32[:]).then_inc(sem.sel_ok, 1)
            steps(0, order(0), first=-1, end=0)
            split_keys(1)
            split_values(1)
            dve.wait_ge(sem.in_small, 16 * 8)
            dve.wait_ge(sem.in_place, 16 * 5)
            tt(m.bgs[:], m.bg0[:, 0, :], m.bg0[:, 1, :], ALU.add)
            steps(0, order(0), first=0)
            table(0)
            dve.memset(m.s2[:, 2, :, :], 0.0)
            keys(1)
            gates(0)
            live_queries()

            def block_step(s, u, first=0, last=2):
                if first <= 0:
                    if s % 8 == 0:
                        expert.extend(eight(mybir.EngineType.DVE, m.blk_e, s, E0N - 1))
                    wait(dve, sem.bh_ps, s - 1)
                    copy(m.w1b[:, u % 2, :], m.w1_0[:, bass.ds(expert[s] * F0, F0)]).then_inc(sem.bw_ok, 1)
                    dve.wait_ge(sem.bx_ps, s + 1)
                    copy(m.place[:, s:s + 1], m.xb[:, u, D:ROW].bitcast(I32)).then_inc(sem.place_ok, 1)
                if first <= 2 <= last:
                    e = expert[s - 2]
                    v = (u - 2) % U
                    dve.wait_ge(sem.by_ps, s - 1)
                    wait(dve, back[0][v], (s - 2 - v) * (16 // U))
                    dve.tensor_tensor(m.yb[:, v, :], m.ps[6 + (u - 2) % 2][:, 0:D],
                                      m.b2_0[:, bass.ds(e * D, D)], ALU.add).then_inc(sem.by_ok, 1)

            dve.wait_ge(sem.in_ffn, 16 * 4 * B)
            dve.wait_ge(sem.table_ok, 1)
            expert = []
            for s in range(NB0 + 2):
                block_step(s, s % U, first=max(0, s - NB0 + 1), last=s)

            dve.wait_ge(sem.live_ok, 4)
            then(stt(m.mb[:], m.keep[:], 1.0, m.live[0:S2, :, :], ALU.subtract, ALU.mult))
            steps(1, order(1))
            table(1)
            gates(1)
            dve.wait_ge(sem.in_w1, 16 * (2 * E1N + 1))
            for e in range(E1N):
                dve.wait_ge(sem.ey_ps, e + 1)
                if e >= 4:
                    dve.wait_ge(back[1][e % 4], 32 * (e // 4))
                for t in range(2):
                    i = tt(m.yb[:, 2 * (e % 4) + t, :], [PJ, PG][e % 2][:, t * P:(t + 1) * P], m.b2_1[:, e * D:(e + 1) * D], ALU.add)
                i.then_inc(sem.ey_ok, 1)
            for b in range(B):
                combine(1, b)

        @block.scalar
        def _(act):
            fn = act.activation

            def copy(o, i):
                return fn(o, i, ACT.Copy)

            def guess(v, n, ready, var):
                ve, ln, g = (x[:, v, n % 2, :] for x in (m.ve, m.ln, m.g))
                act.wait_ge(var, n + 1)
                steps_done[0] += 1
                fn(ln, ve, ACT.Ln).then_inc(sem.a_step, 1)
                act.wait_ge(sem.a_step, steps_done[0])
                fn(g, ln, ACT.Exp, scale=-0.5).then_inc(ready, 1)

            steps_done = [0]

            def guess1(L, b):
                guess(0, B * L + b, sem.guess1, sem.var1)

            def guess2(L, b):
                guess(1, B * L + b, sem.guess2, sem.var2)

            def xnT(L, b):
                n = B * L + b
                act.wait_ge(sem.xn_ps, n + 1)
                wait(act, sem.q_ps, n - 1)
                copy(m.xnT[:, n % 2, :], PM[:, 0:S]).then_inc(sem.xnT_ok, 1)

            def q_high(L, b):
                n = B * L + b
                act.wait_ge(sem.qf_ok if L else sem.q_ps, b + 1 if L else n + 1)
                if n >= 2:
                    act.wait_ge(qst_in[(n - 2) % 3], 16 * NP * ((n - 2) // 3 + 1))
                copy(m.qh[:, n % 2, :], m.qf[:, n % 2, :] if L else PJ[:, 0:S]).then_inc(sem.qh_ok, 1)

            def q_middle(L, b):
                n = B * L + b
                act.wait_ge(sem.qr_ok, n + 1)
                copy(m.qm[:, n % 2, :], m.qr[:, n % 2, :]).then_inc(sem.qm_ok, 1)

            def maxima(L, b):
                n = B * L + b
                act.wait_ge(sem.mx_ps, n + 1)
                wait(act, sem.t_ps, 4 * (n - 1))
                if L == 1:
                    copy(m.rm[0:S2, n % 2, :], m.mb[:, b, :])
                copy(m.rm[64:64 + H, n % 2, :], PG[:].bitcast(BF16)[64:64 + H, S:2 * S]).then_inc(sem.rm_ok, 1)

            def weights(L, b, u):
                n = B * L + b
                act.wait_ge(sem.t_ps, 4 * n + u + 1)
                if u == 0:
                    wait(act, sem.o_ps, n)
                fn(m.pT[:, 2 * u:2 * u + 2, :].rearrange("p c q -> p (c q)"), PT_[u % 2][:], ACT.Exp, scale=SCALE).then_inc(sem.pT_ok, 1)

            def sums(L, b):
                n = B * L + b
                act.wait_ge(sem.o_ps, n + 1)
                wait(act, sem.on_ps, n - 1)
                copy(m.oT[:, n % 2, :, :].rearrange("p g q -> p (g q)"), PO[:]).then_inc(sem.oT_ok, 1)

            def attT(L, b):
                act.wait_ge(sem.at_ps, b + 1)
                wait(act, sem.pj_ps, b - 1)
                copy(m.attT[:, b % 2, :], PM[:, 0:S]).then_inc(sem.attT_ok, 1)

            def xlT(L, b):
                n = B * L + b
                act.wait_ge(sem.xl_ps, n + 1)
                wait(act, sem.lg_ps, n - 1)
                copy(m.xlT[:, n % 2, :], PM[:, 0:S]).then_inc(sem.xlT_ok, 1)

            def order(L):
                return [(xnT, 2), (weights, 0, 0), (weights, 0, 1), (q_high, 2)] + ([(attT, -1)] if L == 0 else []) + [
                    (q_middle, 2), (guess1, 3), (weights, 0, 2), (weights, 0, 3), (guess2, -1), (sums, 0), (xlT, -1), (maxima, 1)]

            def gates(L):
                act.wait_ge(sem.gate_d, L + 1)
                if L == 1:
                    fn(m.wa[:], m.wa[:], ACT.Exp)
                fn(m.wc[:], m.wd[:], ACT.Exp).then_inc(sem.gate_e, 1)

            act.preload_act_table_set("natural_log_exp_and_others")
            for dst, src in ((m.self32[:], a["c_sel"]), (m.hmask[:], a["c_hmask"]), (m.upperf[:], a["c_upper"])):
                act.dma_start(dst, src).then_inc(sem.in_const, 16)
            act.dma_start(m.mi[:], a["mask_1x1xSxS2_ik0"].rearrange("a b q k -> (a b q) k").rearrange("(t p) k -> p t k", p=P)).then_inc(sem.in_mask, 16)
            act.dma_start(m.pi[:], a["mask_Bx1x1xS2_ik0"]).then_inc(sem.in_mask, 16)
            act.wait_ge(sem.ctx_ok, 1)
            for h in range(2):
                i = copy(m.ctxD.rearrange("p b (h k) -> p b h k", h=2)[:, :, h, :], m.ctxT[:].rearrange("p (b k) -> p b k", b=B))
            i.then_inc(sem.ctxD_ok, 1)
            act.wait_ge(sem.sub_ps, 1)
            copy(m.subT[:], PG[0:S2, 0:S]).then_inc(sem.sub_ok, 1)
            steps(0, order(0))
            act.wait_ge(sem.pad_ok, 1)
            pads(act, mybir.EngineType.Activation, 8)
            gates(0)

            def block_step(s, u, first=0, last=1):
                if first <= 0:
                    act.wait_ge(sem.bx_ps, s + 1)
                    wait(act, sem.bh_ps, s - 1)
                    copy(m.xbT[:, u % 2, 0:P], m.ps[u % 2][:, 0:P]).then_inc(sem.bxT_ok, 1)
                if first <= 1 <= last:
                    if (s - 1) % 8 == 0:
                        expert.extend(eight(mybir.EngineType.Activation, m.blk_e, s - 1, E0N - 1))
                    e = expert[s - 1]
                    act.wait_ge(sem.bh_ps, s)
                    wait(act, sem.by_ps, s - 3)
                    for g in range(2):
                        i = fn(m.hT[:, (u - 1) % 2, g * P:(g + 1) * P], m.ps[2 + (u - 1) % 2][:, g * P:(g + 1) * P], ACT.Relu,
                               bias=m.b1_0[:, bass.ds(e, 1), g])
                    i.then_inc(sem.bh_ok, 1)

            act.wait_ge(sem.table_ok, 1)
            expert = []
            for s in range(NB0 + 1):
                block_step(s, s % U, first=max(0, s - NB0 + 1), last=s)

            steps(1, order(1))
            gates(1)

            def expert_x(e):
                act.wait_ge(sem.ex_ps, e + 1)
                wait(act, sem.eh_ps, 4 * (e - 1))
                copy(m.xbT[:, e % 2, :], PM[:, 0:S]).then_inc(sem.exT_ok, 1)

            expert_x(0)
            for e in range(E1N):
                for g in range(4):
                    act.wait_ge(sem.eh_ps, 4 * e + g + 1)
                    if g == 0:
                        wait(act, sem.ey_ps, e - 1)
                    fn(m.hT[:, e % 2, g * S:(g + 1) * S], m.ps[g][:, 0:S], ACT.Gelu_apprx_tanh,
                       bias=m.b1_1[:, e, g:g + 1]).then_inc(sem.ehT_ok, 1)
                if e + 1 < E1N:
                    expert_x(e + 1)

        @block.gpsimd
        def _(pool):
            def send(L):
                for b in range(B):
                    n = B * L + b
                    xl = m.xl[:, n % 2]
                    if L == 0 and b + 2 < B:
                        add_bias(b + 2)
                    pool.wait_ge(sem.xl_ok, n + 1)
                    pool.tensor_copy(xl[:, 1, :, 0:D], xl[:, 0, :, 0:D])
                    pool.tensor_copy(xl[:, :, :, D:ROW].bitcast(I32).rearrange("p k t o -> p k (t o)"),
                                     m.ids[:, 2 * b:2 * b + 2, :].rearrange("p t k -> p k t")).then_inc(sem.g_step, 1)
                    pool.wait_ge(sem.g_step, n + 1)
                    pool.wait_ge(sem.slot_ok, n + 1)
                    for t in range(QT):
                        for k in range(2):
                            pool.indirect_dma_start([xs0, xs1][L], bass.IndirectOffsetOnAxis(ap=m.slot[:, 2 * b + t, k:k + 1], axis=0),
                                                    xl[:, k, t, :], None, bounds_check=(PAD0 if L == 0 else E1N * REG1) - 1,
                                                    oob_is_err=False).then_inc(sent[L][n % 2], 16)

            last_place = pool.to_reg(2 * TOK - 1)

            def return_rows(L, rows, places, done):
                pool.indirect_dma_start(ys[L], bass.IndirectOffsetOnAxis(ap=places.bitcast(U32), axis=0), rows, None,
                                        bounds_check=last_place, oob_is_err=False).then_inc(done, 16)

            pool.memset(vb[0][:], 0.0)
            pool.memset(vb[1][:], 0.0).then_inc(sem.v0_ok, 1)
            pool.wait_ge(sem.v0_ok, 1)
            for v in vb:
                pool.memset(v[0:64, :, :, 16:17], 1.0)
                i = pool.memset(v[64:128, :, :, 17:18], 1.0)
            i.then_inc(sem.vb_ok, 1)
            pool.wait_ge(sem.vb_ok, 1)
            pool.memset(m.zero, 0.0).then_inc(sem.zero_ok, 1)
            pool.wait_ge(sem.keep_ok, 1)
            pool.wait_ge(sem.sub_ok, 1)
            for b in range(B):
                i = pool.tensor_scalar(m.keep[:, b, :], m.subT[:], m.pf[:, b:b + 1], None, ALU.mult)
            i.then_inc(sem.keep_ok, 1)
            pool.wait_ge(sem.in_place, 16 * 5)
            pool.wait_ge(sem.in_small, 16 * 8)

            def add_bias(b):
                pool.wait_ge(sem.xn_ok, b + 1)
                x = m.x[:, 2 * b:2 * b + 2, :]
                pool.tensor_tensor(x, x, m.bp[:].unsqueeze(1).broadcast_to([P, QT, D]), ALU.add).then_inc(sem.xp_ok, 1)

            add_bias(0)
            add_bias(1)
            send(0)
            for j in range(NB0):
                u = j % U
                pool.wait_ge(sem.by_ok, j + 1)
                return_rows(0, m.yb[:, u, :], m.place[:, j:j + 1], back[0][u])
            pool.wait_ge(sem.filled, 16 * (1 + E1N + 4))
            send(1)
            for e in range(E1N):
                pool.wait_ge(sem.ey_ok, e + 1)
                for t in range(2):
                    return_rows(1, m.yb[:, 2 * (e % 4) + t, :], m.xb[:, 2 * e + t, D:ROW], back[1][e % 4])


_DATA = ['x', 'ctx_1024', 'mask_Bx1x1xS2_ik0', 'mask_1x1xSxS2_ik0', 'L0_xattn_Wq', 'L0_xattn_Wk', 'L0_xattn_Wv', 'L0_xattn_Wp',
         'L0_xattn_bp', 'L0_ffn_Wg', 'L0_ffn_bg', 'L0_ffn_bias', 'L0_ffn_W1', 'L0_ffn_b1', 'L0_ffn_W2', 'L0_ffn_b2',
         'L1_xattn_Wq', 'L1_xattn_bq', 'L1_xattn_Wk', 'L1_xattn_bk', 'L1_xattn_Wv', 'L1_xattn_bv', 'L1_ffn_Wg', 'L1_ffn_W1',
         'L1_ffn_b1', 'L1_ffn_W2', 'L1_ffn_b2']


def constants():
    import numpy as np
    sel = np.zeros((80, NC, 2, S2), np.float32)
    for k in range(S2):
        sel[k, :, :, k] = MASK
    for h in range(H):
        sel[64 + h, h // 2, h % 2, :] = -1.0
    p = np.arange(P)
    hmask = np.zeros((KR, 2), np.float32)
    for r in range(KR):
        hmask[r, r % 16 // DH] = 1.0
    ids = (p[:, None, None] + P * np.arange(NT)[None, :, None] + TOK * np.arange(2)[None, None, :]).astype(np.int32)
    side = np.zeros((P, 3, QT, 2), np.float32)
    side[:, 0] = [1.0, -1.0]
    side[:, 1] = [UP0, UP0 - 1.0]
    side[:, 2] = [UP1, UP1 - 1.0]
    pad = np.zeros((P, 2, ROW), np.float32)
    pad.view(np.int32)[:, :, D] = SKIP
    return {"c_ident": np.eye(P, dtype=np.float32), "c_upper": np.triu(np.ones((P, P), np.float32), 1),
            "c_sel": sel.reshape(80, NC * P), "c_hmask": hmask,
            "c_iota": np.tile(np.arange(E0N, dtype=np.float32), (P, 1)), "c_ids": ids, "c_side": side,
            "c_pad": pad.reshape(P, 2 * ROW),
            "c_number": p.astype(np.float32).reshape(P, 1)}


def kernel(**inputs):
    import numpy as np
    import concourse.bacc as bacc
    from concourse.bass_utils import run_bass_kernel_spmd

    nc = bacc.Bacc("TRN2", target_bir_lowering=False, num_devices=1)
    data = {n: np.asarray(inputs[n]) for n in _DATA}
    for w in ("Wq", "Wk", "Wv"):
        data[f"L1_xattn_{w}"] = data[f"L1_xattn_{w}"].T
    for L in (0, 1):
        for w in ("Wq", "Wk"):
            data[f"L{L}_xattn_{w}"] = data[f"L{L}_xattn_{w}"].reshape(D, NC, 2 * DH).transpose(0, 2, 1).reshape(D, D)
    data["c_b1T0"] = data.pop("L0_ffn_b1").reshape(E0N, 2, P).transpose(2, 0, 1)
    data["c_b1T"] = data.pop("L1_ffn_b1").reshape(E1N, 4, P).transpose(2, 0, 1)
    for w in ("bq", "bk"):
        data[f"L1_xattn_{w}"] = data[f"L1_xattn_{w}"].reshape(NC, 2 * DH).T.reshape(P, 1)
    data["mask_Bx1x1xS2_ik0"] = data["mask_Bx1x1xS2_ik0"].reshape(B, S2).T
    data.update(constants())
    arrays = {f"in_{n}": np.ascontiguousarray(v) for n, v in data.items()}
    a = {n: nc.dram_tensor(f"in_{n}", arrays[f"in_{n}"].shape, mybir.dt.from_np(arrays[f"in_{n}"].dtype), kind="ExternalInput").ap()
         for n in data}
    out = nc.dram_tensor("out_0", (B, S, D), F32, kind="ExternalOutput").ap()
    mixture_kernel(nc, a, out)
    r = run_bass_kernel_spmd(nc, [arrays], core_ids=[0])
    return r.results[0]["out_0"]
```

```python
from contextlib import ExitStack

import concourse.bass as bass
from concourse import mybir

ALU = mybir.AluOpType
ACT = mybir.ActivationFunctionType
AX = mybir.AxisListType
F32 = mybir.dt.float32
BF16 = mybir.dt.bfloat16
I32 = mybir.dt.int32
U32 = mybir.dt.uint32

P = 128
B, S, D = 8, 256, 128
S2 = 64
H, DH = 16, 8
TOK = B * S
NT = TOK // P
QT = S // P
NC = H // 2
SCALE = DH ** -0.5
EPS = 1e-5
Q_PART = [0, 0, 0, 1, 1, 2]
K_PART = [0, 1, 2, 0, 1, 0]
NP = len(Q_PART)
KR = NP * 2 * DH
MASK = 2.0 ** 100
E0N, F0 = 16, 256
UP0 = TOK
REG0 = 2 * TOK + P
PAD0 = E0N * REG0
U = 8
NB0 = 2 * TOK // P + E0N
E1N, F1, CAP = 8, 512, 256
UP1 = 2 * CAP
REG1 = 3 * CAP
ROW = D + 1
SKIP = 1 << 20


class Named:
    pass


def tensors(nc, ctx):
    m = Named()

    def sb(name, shape, dt=F32):
        return ctx.enter_context(nc.sbuf_tensor(name, shape, dt))

    m.ident = sb("ident", [P, P])
    m.identb = sb("identb", [P, P], BF16)
    m.upper = sb("upper", [P, P], BF16)
    m.upperf = sb("upperf", [P, P])
    m.onesb = sb("onesb", [P, P], BF16)
    m.sel = sb("sel", [80, NC, P], BF16)
    m.hmask = sb("hmask", [KR, 2])
    m.iota_e = sb("iota_e", [P, E0N])
    m.ids = sb("ids", [P, NT, 2], I32)
    m.side = sb("side", [P, 3, QT, 2])
    m.padrow = sb("padrow", [P, 2 * ROW])
    m.number = sb("number", [P, 1])
    m.wq, m.wk, m.wv = ([sb(f"{w}{L}", [P, P]) for L in (0, 1)] for w in ("wq", "wk", "wv"))
    m.vb = [sb(f"vb{L}", [P, B, NC, 32]) for L in (0, 1)]
    m.kst = sb("kst", [KR, B, NC, 2, S2], BF16)
    m.wp = sb("wp", [P, P])
    m.bp = sb("bp", [P, P])
    m.bq = sb("bq", [P, 1])
    m.bk = sb("bk", [P, 1])
    m.bv = sb("bv", [P, P])
    m.wg0 = sb("wg0", [P, E0N])
    m.bg0 = sb("bg0", [P, 2, E0N])
    m.bgs = sb("bgs", [P, E0N])
    m.wg1 = sb("wg1", [P, E1N])
    m.w1_0 = sb("w1_0", [P, E0N * F0])
    m.w2_0 = sb("w2_0", [P, 2, E0N * D])
    m.b1_0 = sb("b1_0", [P, E0N, 2])
    m.b2_0 = sb("b2_0", [P, E0N * D])
    m.b1_1 = sb("b1_1", [P, E1N, 4])
    m.x = sb("x", [P, NT, D])
    m.ctxr = sb("ctxr", [P, 4, P])
    m.ctxT = sb("ctxT", [P, 512])
    m.kh = sb("kh", [P, 512], BF16)
    m.km = sb("km", [P, 512], BF16)
    m.kl = sb("kl", [P, 512], BF16)
    m.krep = sb("krep", [KR, NC, B, S2], BF16)
    m.mi = sb("mi", [P, 2, S2], I32)
    m.mf = sb("mf", [P, 2, S2])
    m.pi = sb("pi", [S2, B], I32)
    m.pf = sb("pf", [S2, B])
    m.keep = sb("keep", [S2, B, S], BF16)
    m.subT = sb("subT", [S2, S])
    m.live = sb("live", [P, B, S], BF16)
    m.mb = sb("mb", [S2, B, S], BF16)
    m.st = sb("st", [P, 2, 2, QT, 6])
    m.mv = sb("mv", [P, 2, 2, QT, 2])
    m.ve = sb("ve", [P, 2, 2, QT])
    m.ln = sb("ln", [P, 2, 2, QT])
    m.g = sb("g", [P, 2, 2, QT])
    m.t = sb("t", [P, 2, 2, QT])
    m.u = sb("u", [P, 2, 2, QT])
    m.rs = sb("rs", [P, 2, 2, QT])
    m.shift = sb("shift", [P, 2, QT])
    m.xn = sb("xn", [P, 2, QT, D])
    m.xnT = sb("xnT", [P, 2, S])
    m.qf = sb("qf", [P, 2, S])
    m.qr = sb("qr", [P, 2, S])
    m.qh = sb("qh", [P, 2, S], BF16)
    m.qm = sb("qm", [P, 2, S], BF16)
    m.ql = sb("ql", [P, 2, S], BF16)
    m.qst = sb("qst", [KR, 3, NC, S], BF16)
    m.mx = sb("mx", [P, 2, QT, H], BF16)
    m.rm = sb("rm", [80, 2, S], BF16)
    m.pT = sb("pT", [P, NC, S])
    m.oT = sb("oT", [P, 2, 2, S])
    m.rec = sb("rec", [P, 2, 2 * NC, 2])
    m.att = sb("att", [P, 2, 2 * NC, 2, DH])
    m.attT = sb("attT", [P, 2, S])
    m.xl = sb("xl", [P, 2, 2, QT, ROW])
    m.xlT = sb("xlT", [P, 2, S])
    m.lg = sb("lg", [P, NT, E0N])
    m.v8 = sb("v8", [P, NT, 8])
    m.i8 = sb("i8", [P, NT, 8], U32)
    m.oh = sb("oh", [P, 2, QT, 2, E0N], BF16)
    m.s1 = sb("s1", [P, 2, 2, E0N], BF16)
    m.s2 = sb("s2", [P, 3, 2, E0N], BF16)
    m.rt = sb("rt", [P, 2, QT, 2, E0N])
    m.rk = sb("rk", [P, 2, QT, 2])
    m.rb = sb("rb", [P, 2, QT, 2])
    m.ro = sb("ro", [P, 2, QT, 2])
    m.slf = sb("slf", [P, 2, QT, 2])
    m.slot = sb("slot", [P, NT, 2], U32)
    m.wt = sb("wt", [P, 2, NT])
    m.wa = sb("wa", [P, NT, E1N])
    m.wb = sb("wb", [P, NT])
    m.wc = sb("wc", [P, NT])
    m.wd = sb("wd", [P, NT])
    m.we = sb("we", [P, NT])
    m.cnt = sb("cnt", [P, 2, E0N])
    m.tb = sb("tb", [P, 10, E0N])
    m.be = sb("be", [P, 2])
    m.br = sb("br", [P, 2])
    m.bs = sb("bs", [P, 2])
    m.tot = sb("tot", [P, E0N], I32)
    m.toi = sb("toi", [P, E0N], I32)
    m.blk_e = sb("blk_e", [1, NB0], I32)
    m.blk_r = sb("blk_r", [1, NB0], I32)
    m.pad_r = sb("pad_r", [1, E0N], I32)
    m.xb = sb("xb", [P, 2 * E1N, ROW])
    m.xbT = sb("xbT", [P, 2, S])
    m.hb = sb("hb", [P, 2, F0])
    m.hT = sb("hT", [P, 2, 4 * S])
    m.yb = sb("yb", [P, 8, D])
    m.w1b = sb("w1b", [P, 2, F0])
    m.place = sb("place", [P, NB0], I32)
    m.ps = [ctx.enter_context(nc.psum_tensor(f"ps{i}", [P, 512], F32)) for i in range(8)]
    m.w1_1 = m.w1_0[:, :].rearrange("p (e f) -> p e f", e=E1N)
    m.w2_1 = m.w2_0[:, :, :].rearrange("p g (e d) -> p (g e d)", e=E0N).rearrange("p (e g d) -> p e g d", e=E1N, g=4)
    m.b2_1 = m.b2_0[:, 0:E1N * D]
    m.last = m.w1_0[:, :].rearrange("p (k t d) -> p k t d", k=2, d=D)
    m.yl = m.hT[:, 0, :].rearrange("p (n k t d) -> p n k t d", n=2, k=2, t=QT)
    m.zero = m.hT[:, 0, :]
    m.kf = m.xbT[:, :, :].rearrange("p n q -> p (n q)")
    m.kr = m.hb[:, :, :].rearrange("p n q -> p (n q)")
    m.self32 = m.pT[0:80, 0:4, :].rearrange("p c q -> p (c q)")
    m.ctxD = m.pT[:, 4:8, :].rearrange("p c q -> p (c q)").rearrange("p (b k) -> p b k", b=B)
    return m


def mixture_kernel(nc, a, out):
    with ExitStack() as ctx:
        m = tensors(nc, ctx)
        xs0 = nc.dram_tensor("xs0", [PAD0 + P, ROW], F32).ap()
        xs1 = nc.dram_tensor("xs1", [E1N * REG1, ROW], F32).ap()
        ys = [nc.dram_tensor(f"ys{L}", [2 * TOK, D], F32).ap() for L in (0, 1)]
        PA, PT_, PO, PM, PJ, PG = m.ps[0:2], m.ps[2:4], m.ps[4], m.ps[5], m.ps[6], m.ps[7]
        sem = Named()
        sem.in_q = ctx.enter_context(nc.semaphore("in_q"))
        sem.in_l1 = ctx.enter_context(nc.semaphore("in_l1"))
        sem.in_small = ctx.enter_context(nc.semaphore("in_small"))
        sem.zero_ok = ctx.enter_context(nc.semaphore("zero_ok"))
        sem.vb_ok = ctx.enter_context(nc.semaphore("vb_ok"))
        sem.sub_ok = ctx.enter_context(nc.semaphore("sub_ok"))
        sem.xp_ok = ctx.enter_context(nc.semaphore("xp_ok"))
        sem.v0_ok = ctx.enter_context(nc.semaphore("v0_ok"))
        sem.row_ok = ctx.enter_context(nc.semaphore("row_ok"))
        sem.row_ps = ctx.enter_context(nc.semaphore("row_ps"))
        sem.sel_ok = ctx.enter_context(nc.semaphore("sel_ok"))
        sem.ctxD_ok = ctx.enter_context(nc.semaphore("ctxD_ok"))
        sem.in_place = ctx.enter_context(nc.semaphore("in_place"))
        sem.in_const = ctx.enter_context(nc.semaphore("in_const"))
        sem.in_ctx = ctx.enter_context(nc.semaphore("in_ctx"))
        sem.in_mask = ctx.enter_context(nc.semaphore("in_mask"))
        sem.in_ffn = ctx.enter_context(nc.semaphore("in_ffn"))
        sem.in_w1 = ctx.enter_context(nc.semaphore("in_w1"))
        sem.filled = ctx.enter_context(nc.semaphore("filled"))
        sem.v_step = ctx.enter_context(nc.semaphore("v_step"))
        sem.a_step = ctx.enter_context(nc.semaphore("a_step"))
        sem.g_step = ctx.enter_context(nc.semaphore("g_step"))
        sem.ctx_ps = ctx.enter_context(nc.semaphore("ctx_ps"))
        sem.ctx_ok = ctx.enter_context(nc.semaphore("ctx_ok"))
        sem.k_ps = ctx.enter_context(nc.semaphore("k_ps"))
        sem.k_split = ctx.enter_context(nc.semaphore("k_split"))
        sem.krep_in = ctx.enter_context(nc.semaphore("krep_in"))
        sem.kst_ok = ctx.enter_context(nc.semaphore("kst_ok"))
        sem.v_ps = ctx.enter_context(nc.semaphore("v_ps"))
        sem.v_ok = ctx.enter_context(nc.semaphore("v_ok"))
        sem.sub_ps = ctx.enter_context(nc.semaphore("sub_ps"))
        sem.keep_ok = ctx.enter_context(nc.semaphore("keep_ok"))
        sem.live_ps = ctx.enter_context(nc.semaphore("live_ps"))
        sem.live_ok = ctx.enter_context(nc.semaphore("live_ok"))
        sem.var_ok = ctx.enter_context(nc.semaphore("var_ok"))
        sem.guess_ok = ctx.enter_context(nc.semaphore("guess_ok"))
        sem.norm_ok = ctx.enter_context(nc.semaphore("norm_ok"))
        sem.xn_ok = ctx.enter_context(nc.semaphore("xn_ok"))
        sem.xn_ps = ctx.enter_context(nc.semaphore("xn_ps"))
        sem.xnT_ok = ctx.enter_context(nc.semaphore("xnT_ok"))
        sem.q_ps = ctx.enter_context(nc.semaphore("q_ps"))
        sem.qf_ok = ctx.enter_context(nc.semaphore("qf_ok"))
        sem.qh_ok = ctx.enter_context(nc.semaphore("qh_ok"))
        sem.qr_ok = ctx.enter_context(nc.semaphore("qr_ok"))
        sem.qm_ok = ctx.enter_context(nc.semaphore("qm_ok"))
        sem.ql_ok = ctx.enter_context(nc.semaphore("ql_ok"))
        sem.a_ps = ctx.enter_context(nc.semaphore("a_ps"))
        sem.mx_ok = ctx.enter_context(nc.semaphore("mx_ok"))
        sem.mx_ps = ctx.enter_context(nc.semaphore("mx_ps"))
        sem.rm_ok = ctx.enter_context(nc.semaphore("rm_ok"))
        sem.t_ps = ctx.enter_context(nc.semaphore("t_ps"))
        sem.pT_ok = ctx.enter_context(nc.semaphore("pT_ok"))
        sem.o_ps = ctx.enter_context(nc.semaphore("o_ps"))
        sem.oT_ok = ctx.enter_context(nc.semaphore("oT_ok"))
        sem.on_ps = ctx.enter_context(nc.semaphore("on_ps"))
        sem.att_ok = ctx.enter_context(nc.semaphore("att_ok"))
        sem.at_ps = ctx.enter_context(nc.semaphore("at_ps"))
        sem.attT_ok = ctx.enter_context(nc.semaphore("attT_ok"))
        sem.pj_ps = ctx.enter_context(nc.semaphore("pj_ps"))
        sem.x1_ok = ctx.enter_context(nc.semaphore("x1_ok"))
        sem.xl_ok = ctx.enter_context(nc.semaphore("xl_ok"))
        sem.xl_ps = ctx.enter_context(nc.semaphore("xl_ps"))
        sem.xlT_ok = ctx.enter_context(nc.semaphore("xlT_ok"))
        sem.lg_ps = ctx.enter_context(nc.semaphore("lg_ps"))
        sem.oh_ok = ctx.enter_context(nc.semaphore("oh_ok"))
        sem.rank_ps = ctx.enter_context(nc.semaphore("rank_ps"))
        sem.slot_ok = ctx.enter_context(nc.semaphore("slot_ok"))
        sem.own_ok = ctx.enter_context(nc.semaphore("own_ok"))
        sem.cnt_ps = ctx.enter_context(nc.semaphore("cnt_ps"))
        sem.gate_d = ctx.enter_context(nc.semaphore("gate_d"))
        sem.gate_e = ctx.enter_context(nc.semaphore("gate_e"))
        sem.table_ok = ctx.enter_context(nc.semaphore("table_ok"))
        sem.pad_ok = ctx.enter_context(nc.semaphore("pad_ok"))
        sem.padded = ctx.enter_context(nc.semaphore("padded"))
        sem.mbc_ok = ctx.enter_context(nc.semaphore("mbc_ok"))
        sem.bx_ps = ctx.enter_context(nc.semaphore("bx_ps"))
        sem.bxT_ok = ctx.enter_context(nc.semaphore("bxT_ok"))
        sem.place_ok = ctx.enter_context(nc.semaphore("place_ok"))
        sem.bh_ps = ctx.enter_context(nc.semaphore("bh_ps"))
        sem.bw_ok = ctx.enter_context(nc.semaphore("bw_ok"))
        sem.bh_ok = ctx.enter_context(nc.semaphore("bh_ok"))
        sem.by_ps = ctx.enter_context(nc.semaphore("by_ps"))
        sem.by_ok = ctx.enter_context(nc.semaphore("by_ok"))
        sem.ex_ps = ctx.enter_context(nc.semaphore("ex_ps"))
        sem.exT_ok = ctx.enter_context(nc.semaphore("exT_ok"))
        sem.eh_ps = ctx.enter_context(nc.semaphore("eh_ps"))
        sem.ehT_ok = ctx.enter_context(nc.semaphore("ehT_ok"))
        sem.ey_ps = ctx.enter_context(nc.semaphore("ey_ps"))
        sem.ey_ok = ctx.enter_context(nc.semaphore("ey_ok"))
        sem.weights_ok = ctx.enter_context(nc.semaphore("weights_ok"))
        sem.scaled = ctx.enter_context(nc.semaphore("scaled"))
        sem.second_ok = ctx.enter_context(nc.semaphore("second_ok"))
        sem.xo_ok = ctx.enter_context(nc.semaphore("xo_ok"))
        sem.stored = ctx.enter_context(nc.semaphore("stored"))

        def sems(name, n):
            return [ctx.enter_context(nc.semaphore(f"{name}{i}")) for i in range(n)]

        in_x, window_in, last_in = sems("in_x", 4), sems("window_in", E1N), [sems("first_in", 4), sems("second_in", 4)]
        qst_in, yl_in, xb_in = sems("qst_in", 3), sems("yl_in", 2), sems("xb_in", U)
        sent = [sems("sent_a", 2), sems("sent_b", 2)]
        back = [sems("back_a", U), sems("back_b", 4)]
        wq, wk, wv, vb = m.wq, m.wk, m.wv, m.vb
        EN = [E0N, E1N]
        block = ctx.enter_context(nc.Block())

        def wait(eng, which, value):
            if not isinstance(value, int) or value > 0:
                eng.wait_ge(which, value)

        def eight(engine, table, j, top):
            return nc.values_load_multi_w_load_instructions(
                table[0:1, j:j + 8], engines=[engine], min_val=0, max_val=top,
                skip_runtime_bounds_check_because="table() bounds them")[1]

        def pads(eng, engine, e):
            for r in eight(engine, m.pad_r, e, PAD0):
                eng.dma_start(xs0[bass.ds(r, P), :], m.padrow[:, 0:ROW]).then_inc(sem.padded, 16)

        def halves(i):
            return slice(0 if i + 3 < B else 1, 2 if i >= 1 else 1)

        def steps(L, order, first=-3, end=B + 2):
            for i in range(first, end):
                for stage, lead, *more in order:
                    if lead is None:
                        stage(L, i)
                    elif 0 <= i + lead < B:
                        stage(L, i + lead, *more)

        def store(sp, b):
            sp.wait_ge(sem.xo_ok, b + 1)
            sp.dma_start(out.rearrange("b s d -> (b s) d")[b * S:(b + 1) * S, :].rearrange("(t p) d -> p t d", p=P),
                         m.x[:, 2 * b:2 * b + 2, :]).then_inc(sem.stored, 16)

        @block.sync
        def _(sp):
            def load_x(g):
                sp.dma_start(m.x[:, 4 * g:4 * g + 4, :], a["x"].rearrange("b s d -> (b s) d")[2 * g * S:2 * (g + 1) * S, :]
                             .rearrange("(t p) d -> p t d", p=P)).then_inc(in_x[g], 16)

            for dst, src in ((m.ident[:], a["c_ident"]),
                             (m.ctxr[:], a["ctx_1024"].rearrange("b k d -> (b k) d").rearrange("(t p) d -> p t d", p=P)),
                             (wk[0][:], a["L0_xattn_Wk"])):
                sp.dma_start(dst, src).then_inc(sem.in_ctx, 16)
            load_x(0)
            sp.dma_start(wq[0][:], a["L0_xattn_Wq"]).then_inc(sem.in_q, 16)
            sp.dma_start(wv[0][:], a["L0_xattn_Wv"]).then_inc(sem.in_q, 16)

            def ffn_weights(L, b):
                E, EE = slice(2 * b, 2 * b + 2), 2 * b
                for dst, src in ((m.w1_0[:, EE * F0:(EE + 2) * F0].rearrange("p (e f) -> p e f", e=2), a["L0_ffn_W1"][E].rearrange("e d f -> d e f")),
                                 (m.w2_0[:, 0, EE * D:(EE + 2) * D].rearrange("p (e d) -> p e d", e=2), a["L0_ffn_W2"][E, 0:P, :].rearrange("e f d -> f e d")),
                                 (m.w2_0[:, 1, EE * D:(EE + 2) * D].rearrange("p (e d) -> p e d", e=2), a["L0_ffn_W2"][E, P:2 * P, :].rearrange("e f d -> f e d")),
                                 (m.b2_0[:, EE * D:(EE + 2) * D], a["L0_ffn_b2"][E].rearrange("e d -> (e d)").partition_broadcast(P))):
                    sp.dma_start(dst, src).then_inc(sem.in_ffn, 16)

            def fill(L, b):
                if b == 0:
                    sp.wait_ge(sem.in_place, 16 * 5)
                    sp.wait_ge(sem.zero_ok, 1)
                    sp.dma_start(xs0[PAD0:PAD0 + P, :], m.padrow[:, 0:ROW]).then_inc(sem.filled, 16)
                sp.dma_start(xs1[b * REG1 + CAP:b * REG1 + 2 * CAP, :].rearrange("(p r) d -> p (r d)", r=2),
                             m.padrow[:]).then_inc(sem.filled, 16)
                if b % 2:
                    i = b // 2
                    sp.dma_start(ys[1][i * 1024:(i + 1) * 1024, :].rearrange("(p r) d -> p (r d)", r=8),
                                 m.zero).then_inc(sem.filled, 16)

            def k_rows(L):
                for i, part in enumerate(K_PART):
                    sp.wait_ge(sem.k_split, 3 * L + part + 1)
                    if i == 0 and L == 1:
                        sp.wait_ge(sem.kst_ok, 1)
                    sp.dma_start(m.krep[16 * i:16 * i + 16, :, :, :].rearrange("r c b k -> r c (b k)"),
                                 [m.kh, m.km, m.kl][part][:, :]).then_inc(sem.krep_in, 16)

            k_rows(0)
            load_x(1)
            for dst, src in ((m.ids[:], a["c_ids"]), (m.side[:], a["c_side"]), (m.padrow[:], a["c_pad"]),
                             (m.iota_e[:], a["c_iota"]), (m.number[:], a["c_number"])):
                sp.dma_start(dst, src).then_inc(sem.in_place, 16)

            def q_rows(L, b):
                n = B * L + b
                src, ready = [m.qh, m.qm, m.ql], [sem.qh_ok, sem.qm_ok, sem.ql_ok]
                if n >= 3:
                    sp.wait_ge(sem.t_ps, 4 * (n - 2))
                for i, part in enumerate(Q_PART):
                    sp.wait_ge(ready[part], n + 1)
                    sp.dma_start(m.qst[16 * i:16 * i + 16, n % 3, :, :], src[part][:, n % 2, :]).then_inc(qst_in[n % 3], 16)

            def back_rows(L, b):
                n = B * L + b
                if b == 0:
                    for done in back[0]:
                        sp.wait_ge(done, 16 * NB0 // U)
                if n >= 2:
                    sp.wait_ge(sem.mbc_ok, n - 1)
                for k in range(2):
                    sp.dma_start(m.yl[:, n % 2, k, :, :],
                                 ys[L][k * TOK + b * S:k * TOK + (b + 1) * S, :].rearrange("(t p) d -> p t d", p=P)
                                 ).then_inc(yl_in[n % 2], 16)

            steps(0, [(q_rows, 2)], end=-1)
            for dst, src in ((wk[1][:], a["L1_xattn_Wk"]), (wv[1][:], a["L1_xattn_Wv"]), (m.bk[:], a["L1_xattn_bk"]),
                             (m.bv[:], a["L1_xattn_bv"].partition_broadcast(P)), (m.bq[:], a["L1_xattn_bq"]), (wq[1][:], a["L1_xattn_Wq"])):
                sp.dma_start(dst, src).then_inc(sem.in_l1, 16)
            for dst, src in ((m.bp[:], a["L0_xattn_bp"].partition_broadcast(P)), (m.wp[:], a["L0_xattn_Wp"]),
                             (m.wg0[:], a["L0_ffn_Wg"]), (m.bg0[:, 0, :], a["L0_ffn_bg"].partition_broadcast(P)),
                             (m.bg0[:, 1, :], a["L0_ffn_bias"].partition_broadcast(P)), (m.wg1[:], a["L1_ffn_Wg"]),
                             (m.b1_1[:], a["c_b1T"]), (m.b1_0[:], a["c_b1T0"])):
                sp.dma_start(dst, src).then_inc(sem.in_small, 16)
            load_x(2)
            steps(0, [(q_rows, 2)], first=-1, end=0)
            k_rows(1)
            load_x(3)
            steps(0, [(q_rows, 2), (ffn_weights, 0), (fill, 0)], first=0)
            sp.wait_ge(sem.pad_ok, 1)
            pads(sp, mybir.EngineType.SP, 0)
            sp.wait_ge(sem.table_ok, 1)
            for done in sent[0]:
                sp.wait_ge(done, 16 * NT)
            sp.wait_ge(sem.padded, 16 * E0N)
            sp.wait_ge(sem.filled, 16 * (1 + E1N + 4))

            def load_block(j, u, wait):
                if u == 0:
                    row[:] = eight(mybir.EngineType.SP, m.blk_r, j, PAD0)
                r = row[u]
                if wait is not None:
                    sp.wait_ge(sem.place_ok, wait)
                sp.dma_start(m.xb[:, u, :], xs0[bass.ds(r, P), :]).then_inc(xb_in[u], 16)

            row = []
            for j in range(NB0):
                load_block(j, j % U, j - U + 1 if j >= U else None)

            sp.wait_ge(sem.by_ok, NB0)

            def first_results(L, b):
                back_rows(0, b)

            def expert_weights(L, e):
                sp.dma_start(m.w1_1[:, e, :], a["L1_ffn_W1"][e]).then_inc(sem.in_w1, 16)
                sp.dma_start(m.w2_1[:, e, :, :], a["L1_ffn_W2"][e].rearrange("(c p) d -> p c d", p=P)).then_inc(sem.in_w1, 16)
                if e == 0:
                    sp.dma_start(m.b2_1, a["L1_ffn_b2"].rearrange("e d -> (e d)").partition_broadcast(P)).then_inc(sem.in_w1, 16)

            steps(1, [(first_results, 4), (q_rows, 2), (expert_weights, 0)], first=-4)
            sp.wait_ge(sem.table_ok, 2)
            for done in sent[1]:
                sp.wait_ge(done, 16 * NT)
            row = eight(mybir.EngineType.SP, m.blk_r, 0, E1N * REG1 - CAP)
            for e in range(E1N):
                for h in range(2):
                    sp.dma_start(m.xb[:, 2 * e + h, :], xs1[bass.ds(row[e] + h * P, P), :]).then_inc(window_in[e], 16)
            for done in back[1]:
                sp.wait_ge(done, 16 * 2 * E1N // len(back[1]))
            for g in range(B // 2):
                for k in (1, 0):
                    sp.dma_start(m.last[:, k, 4 * g:4 * g + 4, :],
                                 ys[1][k * TOK + 2 * g * S:k * TOK + 2 * (g + 1) * S, :].rearrange("(t p) d -> p t d", p=P)
                                 ).then_inc(last_in[k][g], 16)
            for b in range(B - 1):
                store(sp, b)
            store(sp, B - 1)
            sp.wait_ge(sem.stored, 16 * B)

        @block.tensor
        def _(pe):
            mm = pe.matmul
            pe.wait_ge(sem.in_ctx, 16 * 3)
            for t in range(4):
                i = pe.transpose(PA[0][:, t * P:(t + 1) * P], m.ctxr[:, t, :], m.ident[:])
            i.then_inc(sem.ctx_ps, 1)
            pe.wait_ge(sem.ctx_ok, 1)
            mm(PA[1][:, :], wk[0][:], m.ctxT[:]).then_inc(sem.k_ps, 1)
            pe.wait_ge(sem.in_q, 32)
            pe.wait_ge(sem.ctxD_ok, 1)
            for g in range(2):
                for b in range(4):
                    i = mm(PT_[g][:, b * P:(b + 1) * P], m.ctxD[:, 4 * g + b, :], wv[0][:])
                i.then_inc(sem.v_ps, 1)
            pe.wait_ge(sem.keep_ok, 1)
            for t in range(2):
                i = pe.transpose(PG[0:S2, t * P:(t + 1) * P], m.mf[:, t, :], m.ident[:])
            i.then_inc(sem.sub_ps, 1)

            def second_keys():
                pe.wait_ge(sem.in_l1, 16 * 6)
                pe.wait_ge(sem.v_ok, 2)
                mm(PT_[0][:, :], wk[1][:], m.ctxT[:]).then_inc(sem.k_ps, 1)
                for g in range(2):
                    for b in range(4):
                        i = mm([PT_[1], PO][g][:, b * P:(b + 1) * P], m.ctxD[:, 4 * g + b, :], wv[1][:])
                    i.then_inc(sem.v_ps, 1)

            def live_keys():
                pe.wait_ge(sem.keep_ok, 2)
                for g in range(4):
                    mm([PA[0], PA[1], PT_[0], PT_[1]][g][:], m.onesb[0:S2, :], m.keep[:, 2 * g:2 * g + 2, :]).then_inc(sem.live_ps, 1)

            def block_rows():
                pe.wait_ge(sem.row_ok, 1)
                mm(PG[0:1, 0:NB0], m.be[0:NB0, 0:1], m.ident[0:NB0, 0:NB0])
                mm(PG[0:1, NB0:2 * NB0], m.br[0:NB0, 1:2], m.ident[0:NB0, 0:NB0]).then_inc(sem.row_ps, 1)

            read = {"PM": None, "PJ": None, "PG": (sem.sub_ok, 1)}

            def after_read(bank):
                if read[bank]:
                    pe.wait_ge(read[bank][0], read[bank][1])

            def xn_transpose(L, b):
                n = B * L + b
                pe.wait_ge(sem.xn_ok, n + 1)
                after_read("PM")
                read["PM"] = (sem.xnT_ok, n + 1)
                for t in range(QT):
                    i = pe.transpose(PM[:, t * P:(t + 1) * P], m.xn[:, n % 2, t, :], m.ident[:])
                i.then_inc(sem.xn_ps, 1)

            def q_product(L, b):
                n = B * L + b
                if n == 0:
                    pe.wait_ge(sem.in_q, 32)
                pe.wait_ge(sem.xnT_ok, n + 1)
                after_read("PJ")
                read["PJ"] = (sem.qf_ok, b + 1) if L else (sem.qr_ok, n + 1)
                mm(PJ[:, 0:S], wq[L][:], m.xnT[:, n % 2, :]).then_inc(sem.q_ps, 1)

            def scores(L, b, u):
                n, t, g = B * L + b, u // 2, u % 2
                if u == 0:
                    pe.wait_ge(sem.kst_ok, L + 1)
                    pe.wait_ge(qst_in[n % 3], 16 * NP * (n // 3 + 1))
                if 4 * n + u >= 2:
                    pe.wait_ge(sem.mx_ok, 4 * n + u - 1)
                o = PA[u % 2]
                if L == 1:
                    mm(o[:, :], m.mb[:, b, t * P:(t + 1) * P], m.sel[0:S2, 0:4, :], start=True, stop=False,
                       skip_group_check=True)
                for c in range(4):
                    i = mm(o[:, c * P:(c + 1) * P], m.qst[:, n % 3, 4 * g + c, t * P:(t + 1) * P],
                           m.kst[:, b, 4 * g + c, :, :], start=(L == 0), stop=True, skip_group_check=True)
                i.then_inc(sem.a_ps, 1)

            def max_transpose(L, b):
                n = B * L + b
                pe.wait_ge(sem.mx_ok, 4 * n + 4)
                pe.wait_ge(sem.sel_ok, 1)
                after_read("PG")
                read["PG"] = (sem.rm_ok, n + 1)
                for t in range(QT):
                    i = pe.transpose(PG[:, :].bitcast(BF16)[64:64 + H, S + t * P:S + (t + 1) * P], m.mx[:, n % 2, t, :], m.identb[:])
                i.then_inc(sem.mx_ps, 1)

            def scores_T(L, b, u):
                n = B * L + b
                if u == 0:
                    pe.wait_ge(sem.rm_ok, n + 1)
                if n == 0 and u < 2:
                    if u == 0:
                        pe.wait_ge(sem.k_split, 4)
                    else:
                        pe.wait_ge(sem.v_ok, 3)
                if 4 * n + u >= 2:
                    pe.wait_ge(sem.pT_ok, 4 * n + u - 1)
                for c in range(2):
                    o = PT_[u % 2][:, c * S:(c + 1) * S]
                    mm(o, m.sel[:, 2 * u + c, :], m.rm[:, n % 2, :], start=(c == 0), stop=False, skip_group_check=True)
                    i = mm(o, m.kst[:, b, 2 * u + c, :, :], m.qst[:, n % 3, 2 * u + c, :], start=False, stop=True,
                           skip_group_check=True)
                i.then_inc(sem.t_ps, 1)

            def values(L, b):
                n = B * L + b
                if n == 0:
                    pe.wait_ge(sem.v_ok, 4)
                pe.wait_ge(sem.pT_ok, 4 * n + 4)
                if n >= 1:
                    pe.wait_ge(sem.att_ok, n)
                for c in range(NC):
                    r = 32 * (c % 4)
                    i = mm(PO[r:r + 32, (c // 4) * S:(c // 4 + 1) * S], vb[L][:, b, c, :], m.pT[:, c, :])
                i.then_inc(sem.o_ps, 1)

            def o_transpose(L, b):
                n = B * L + b
                pe.wait_ge(sem.oT_ok, n + 1)
                for t in range(QT):
                    for g in range(2):
                        i = pe.transpose(PO[:, (2 * t + g) * P:(2 * t + g + 1) * P], m.oT[:, n % 2, g, t * P:(t + 1) * P], m.ident[:])
                i.then_inc(sem.on_ps, 1)

            def att_transpose(L, b):
                pe.wait_ge(sem.att_ok, b + 1)
                after_read("PM")
                read["PM"] = (sem.attT_ok, b + 1)
                for t in range(QT):
                    i = pe.transpose(PM[:, t * P:(t + 1) * P], m.att[:, b % 2, 8 * t:8 * t + 8, :, :], m.ident[:])
                i.then_inc(sem.at_ps, 1)

            def project(L, b):
                pe.wait_ge(sem.in_small, 16 * 8)
                pe.wait_ge(sem.attT_ok, b + 1)
                after_read("PJ")
                read["PJ"] = (sem.x1_ok, b + 1)
                for t in range(QT):
                    i = mm(PJ[:, t * P:(t + 1) * P], m.attT[:, b % 2, t * P:(t + 1) * P], m.wp[:])
                i.then_inc(sem.pj_ps, 1)

            def xl_transpose(L, b):
                n = B * L + b
                pe.wait_ge(sem.xl_ok, n + 1)
                after_read("PM")
                read["PM"] = (sem.xlT_ok, n + 1)
                for t in range(QT):
                    i = pe.transpose(PM[:, t * P:(t + 1) * P], m.xl[:, n % 2, 0, t, 0:D], m.ident[:])
                i.then_inc(sem.xl_ps, 1)

            def router(L, b):
                n = B * L + b
                pe.wait_ge(sem.xlT_ok, n + 1)
                after_read("PG")
                read["PG"] = (sem.oh_ok, n + 1)
                for t in range(QT):
                    o = PG[:, t * EN[L]:(t + 1) * EN[L]]
                    i = mm(o, m.xlT[:, n % 2, t * P:(t + 1) * P], [m.wg0, m.wg1][L][:])
                i.then_inc(sem.lg_ps, 1)

            def ranks(L, b):
                n, w = B * L + b, 2 * EN[L]
                pe.wait_ge(sem.oh_ok, n + 1)
                after_read("PG")
                read["PG"] = (sem.own_ok, n + 1)
                o = [PG[:, 64 + t * w:64 + (t + 1) * w] for t in range(QT)]
                oh = [m.oh[:, n % 2, t, :, 0:EN[L]] for t in range(QT)]
                mm(o[0], m.upper[:], oh[0], start=True, stop=False, skip_group_check=True)
                mm(o[0], m.onesb[:], m.s2[:, (b + 2) % 3, :, 0:EN[L]], start=False, stop=True, skip_group_check=True)
                mm(o[1], m.upper[:], oh[1], start=False, stop=False, skip_group_check=True)
                mm(o[1], m.onesb[:], m.s1[:, n % 2, :, 0:EN[L]], start=False, stop=True, skip_group_check=True).then_inc(sem.rank_ps, 1)

            def counts(L):
                pe.wait_ge(sem.slot_ok, B * (L + 1))
                mm(PG[:, 0:2 * EN[L]], m.onesb[:], m.s2[:, (B - 1) % 3, :, 0:EN[L]]).then_inc(sem.cnt_ps, 1)

            def order(L):
                o = [(scores_T, 0, 0), (scores, 1, 0), (scores, 1, 1), (xn_transpose, 2), (scores_T, 0, 1), (q_product, 2), (scores, 1, 2)]
                if L == 0:
                    o += [(att_transpose, -1), (scores_T, 0, 2), (ranks, -2), (scores, 1, 3), (project, -1)]
                else:
                    o += [(scores_T, 0, 2), (ranks, -2), (scores, 1, 3)]
                return o + [(scores_T, 0, 3), (max_transpose, 1), (values, 0), (xl_transpose, -1), (o_transpose, 0), (router, -1)]

            steps(0, order(0), end=0)
            second_keys()
            steps(0, order(0), first=0)
            counts(0)
            live_keys()
            block_rows()
            pe.wait_ge(sem.live_ok, 4)

            def block_step(s, u, first=0, last=2):
                if first <= 0:
                    wait(pe, sem.bxT_ok, s - 1)
                    pe.wait_ge(xb_in[u], (s - u) * (16 // U) + 16)
                    pe.transpose(m.ps[u % 2][:, 0:P], m.xb[:, u, 0:D], m.ident[:]).then_inc(sem.bx_ps, 1)
                if first <= 1 <= last:
                    pe.wait_ge(sem.bxT_ok, s)
                    pe.wait_ge(sem.bw_ok, s)
                    wait(pe, sem.bh_ok, s - 2)
                    for g in range(2):
                        i = pe.matmul(m.ps[2 + (u - 1) % 2][:, g * P:(g + 1) * P], m.w1b[:, (u - 1) % 2, g * P:(g + 1) * P],
                                      m.xbT[:, (u - 1) % 2, 0:P])
                    i.then_inc(sem.bh_ps, 1)
                if first <= 2 <= last:
                    if (s - 2) % 8 == 0:
                        expert.extend(eight(mybir.EngineType.PE, m.blk_e, s - 2, E0N - 1))
                    e = expert[s - 2]
                    pe.wait_ge(sem.bh_ok, s - 1)
                    wait(pe, sem.by_ok, s - 3)
                    for g in range(2):
                        i = pe.matmul(m.ps[6 + (u - 2) % 2][:, 0:D], m.hT[:, (u - 2) % 2, g * P:(g + 1) * P],
                                      m.w2_0[:, g, bass.ds(e * D, D)], start=(g == 0), stop=(g == 1))
                    i.then_inc(sem.by_ps, 1)

            pe.wait_ge(sem.table_ok, 1)
            pe.wait_ge(sem.in_ffn, 16 * 4 * B)
            expert = []
            for s in range(NB0 + 2):
                block_step(s, s % U, first=max(0, s - NB0 + 1), last=s)
            pe.wait_ge(sem.by_ok, NB0)

            steps(1, order(1))
            counts(1)

            def expert_x(e):
                pe.wait_ge(window_in[e], 32)
                if e >= 1:
                    pe.wait_ge(sem.exT_ok, e)
                for t in range(2):
                    i = pe.transpose(PM[:, t * P:(t + 1) * P], m.xb[:, 2 * e + t, 0:D], m.ident[:])
                i.then_inc(sem.ex_ps, 1)

            def expert_h(e):
                pe.wait_ge(sem.exT_ok, e + 1)
                for g in range(4):
                    if 4 * e + g >= 4:
                        pe.wait_ge(sem.ehT_ok, 4 * e + g - 3)
                    mm(m.ps[g][:, 0:S], m.w1_1[:, e, g * P:(g + 1) * P], m.xbT[:, e % 2, :]).then_inc(sem.eh_ps, 1)

            def expert_y(e):
                if e >= 2:
                    pe.wait_ge(sem.ey_ok, e - 1)
                o = [PJ, PG][e % 2]
                pe.wait_ge(sem.ehT_ok, 4 * e + 4)
                for t in range(2):
                    for g in range(4):
                        i = mm(o[:, t * P:(t + 1) * P], m.hT[:, e % 2, g * S + t * P:g * S + (t + 1) * P], m.w2_1[:, e, g, :],
                               start=(g == 0), stop=(g == 3))
                i.then_inc(sem.ey_ps, 1)

            pe.wait_ge(sem.table_ok, 2)
            pe.wait_ge(sem.in_w1, 16 * (2 * E1N + 1))
            expert_x(0)
            for e in range(E1N + 1):
                if e < E1N:
                    expert_h(e)
                if e + 1 < E1N:
                    expert_x(e + 1)
                if e >= 1:
                    expert_y(e - 1)

        @block.vector
        def _(dve):
            done = [0]

            def then(i):
                done[0] += 1
                i.then_inc(sem.v_step, 1)
                dve.wait_ge(sem.v_step, done[0])

            tt, ts, stt, copy = dve.tensor_tensor, dve.tensor_scalar, dve.scalar_tensor_tensor, dve.tensor_copy
            dve.memset(m.onesb[:], 1.0)
            dve.memset(m.rm[:], 0.0)
            dve.memset(m.s2[:], 0.0)
            dve.wait_ge(sem.ctx_ps, 1)
            copy(m.ctxT[:], PA[0][:]).then_inc(sem.ctx_ok, 1)

            def keys(L):
                dve.wait_ge(sem.krep_in, 16 * NP * (L + 1))
                if L == 1:
                    dve.wait_ge(sem.t_ps, 4 * B)
                for h in range(2):
                    i = ts(m.kst[:, :, :, h, :], m.krep[:].rearrange("r c b k -> r b c k"), m.hmask[:, h:h + 1], None, ALU.mult)
                i.then_inc(sem.kst_ok, 1)

            def split_keys(L):
                if L == 1:
                    dve.wait_ge(sem.in_l1, 16 * 6)
                    dve.wait_ge(sem.krep_in, 16 * NP)
                dve.wait_ge(sem.k_ps, L + 1)
                then(ts(m.kf[:], [PA[1], PT_[0]][L][:], m.bk[:, 0:1] if L else 0.0, None, ALU.add))
                copy(m.kh[:], m.kf[:]).then_inc(sem.k_split, 1)
                dve.wait_ge(sem.k_split, 3 * L + 1)
                then(tt(m.kr[:], m.kf[:], m.kh[:], ALU.subtract))
                copy(m.km[:], m.kr[:]).then_inc(sem.k_split, 1)
                dve.wait_ge(sem.k_split, 3 * L + 2)
                tt(m.kl[:], m.kr[:], m.km[:], ALU.subtract).then_inc(sem.k_split, 1)

            def split_values(L):
                if L == 1:
                    dve.wait_ge(sem.in_l1, 16 * 6)
                for g in range(2):
                    dve.wait_ge(sem.v_ps, 2 * L + g + 1)
                    for h in range(2):
                        rows = slice(64 * h, 64 * h + 64)
                        src = [PT_[0], PT_[1], PT_[1], PO][2 * L + g][rows, :].rearrange("p (b c h d) -> p b c h d", b=4, c=NC, h=2)[:, :, :, h, :]
                        dst = vb[L][rows, 4 * g:4 * g + 4, :, 8 * h:8 * h + 8]
                        if L == 0:
                            i = copy(dst, src)
                        else:
                            bv = m.bv[rows, :].rearrange("p (c h d) -> p c h d", c=NC, h=2)[:, :, h, :]
                            i = tt(dst, src, bv.unsqueeze(1).broadcast_to([64, 4, NC, DH]), ALU.add)
                    i.then_inc(sem.v_ok, 1)

            def live_queries():
                for g in range(4):
                    dve.wait_ge(sem.live_ps, g + 1)
                    ts(m.live[:, 2 * g:2 * g + 2, :], [PA[0], PA[1], PT_[0], PT_[1]][g][:].rearrange("p (b q) -> p b q", b=2), 1.0, None,
                       ALU.min).then_inc(sem.live_ok, 1)

            def mark(i):
                done[0] += 1
                i.then_inc(sem.v_step, 1)
                return done[0]

            def need(number):
                dve.wait_ge(sem.v_step, number)

            def on(b):
                return 0 <= b < B

            def maximum(L, b, u):
                n = B * L + b
                dve.wait_ge(sem.a_ps, 4 * n + u + 1)
                if u == 0:
                    wait(dve, sem.mx_ps, n - 1)
                dve.tensor_reduce(m.mx[:, n % 2, u // 2, 8 * (u % 2):8 * (u % 2) + 8],
                                  PA[u % 2][:].rearrange("p (h k) -> p h k", h=8), AX.X, ALU.max).then_inc(sem.mx_ok, 1)

            def add_result(L, b, k):
                for t in range(QT):
                    x = m.x[:, 2 * b + t, :]
                    y = m.yl[:, b % 2, k, t, :] if L == 0 else m.last[:, k, 2 * b + t, :]
                    i = stt(x, y, m.wt[:, k, 2 * b + t:2 * b + t + 1], x, ALU.mult, ALU.add)
                return i

            def moments(v, n, b):
                for t in range(QT):
                    i = dve.bn_stats(m.st[:, v, n % 2, t, :], m.x[:, 2 * b + t, :])
                return mark(i)

            def mean_variance(v, n):
                for t in range(QT):
                    i = dve.bn_aggr(m.mv[:, v, n % 2, t, :], m.st[:, v, n % 2, t, :])
                return mark(i)

            def iteration(L, i):
                done_, add, scored, query, fresh = i - 2, i - 1, i + 1, i + 2, i + 3
                E = EN[L]
                nd, na, nq, nf = (B * L + b for b in (done_, add, query, fresh))
                rank = PG[:, 64:64 + 4 * E].rearrange("p (t k e) -> p t k e", t=QT, k=2)
                rt, rk, rb, ro, slf = (x[:, nd % 2] for x in (m.rt, m.rk, m.rb, m.ro, m.slf))
                tiles = slice(2 * done_, 2 * done_ + 2)
                o = PO[:].rearrange("p (g j) -> p g j", j=32)
                if on(fresh):
                    if L == 0:
                        dve.wait_ge(in_x[fresh // 2], 16)
                        moment = moments(0, nf, fresh)
                    else:
                        dve.wait_ge(yl_in[fresh % 2], 32 * (fresh // 2 + 1))
                        one = mark(add_result(0, fresh, 0))
                if on(fresh) and L == 1:
                    need(one)
                    add_result(0, fresh, 1).then_inc(sem.mbc_ok, 1)
                if on(fresh) and L == 1:
                    dve.wait_ge(sem.mbc_ok, fresh + 1)
                    moment = moments(0, nf, fresh)
                if on(fresh):
                    need(moment)
                    fresh_mv = mean_variance(0, nf)
                if on(add):
                    dve.wait_ge(sem.on_ps, na + 1)
                    sums = mark(dve.reciprocal(m.rec[:, na % 2, :, :], o[:, :, 16:18]))
                if on(add):
                    need(sums)
                    if L == 0:
                        wait(dve, sem.at_ps, na - 1)
                    tt(m.att[:, na % 2, :, :, :], o[:, :, 0:16].rearrange("p g (h d) -> p g h d", h=2),
                       m.rec[:, na % 2, :, :].unsqueeze(3).broadcast_to([P, 16, 2, DH]), ALU.mult).then_inc(sem.att_ok, 1)
                if on(done_):
                    dve.wait_ge(sem.lg_ps, nd + 1)
                    lg, src = m.lg[:, tiles, 0:E], PG[:, 0:2 * E].rearrange("p (t e) -> p t e", t=QT)
                    logits = mark(copy(lg, src) if L else tt(lg, src, m.bgs[:].unsqueeze(1).broadcast_to([P, QT, E]), ALU.add))
                if on(done_):
                    need(logits)
                    for t in range(2 * done_, 2 * done_ + 2):
                        j = dve.max(m.v8[:, t, :], m.lg[:, t, 0:E])
                    top = mark(j)
                if on(done_):
                    need(top)
                    for t in range(2 * done_, 2 * done_ + 2):
                        j = dve.max_index(m.i8[:, t, :], m.v8[:, t, :], m.lg[:, t, 0:E])
                    index = mark(j)
                if on(scored):
                    maximum(L, scored, 0)
                if on(done_):
                    need(index)
                    wait(dve, sem.rank_ps, nd - 1)
                    hot = mark(tt(m.oh[:, nd % 2, :, :, 0:E], m.iota_e[:, 0:E].unsqueeze(1).unsqueeze(1).broadcast_to([P, QT, 2, E]),
                                  m.i8[:, tiles, 0:2].unsqueeze(3).broadcast_to([P, QT, 2, E]), ALU.is_equal))
                if on(scored):
                    maximum(L, scored, 1)
                if on(done_):
                    need(hot)
                    count = mark(tt(m.s1[:, nd % 2, :, 0:E], m.s2[:, (done_ + 2) % 3, :, 0:E], m.oh[:, nd % 2, 0, :, 0:E], ALU.add))
                if on(query) and L == 1:
                    dve.wait_ge(sem.q_ps, nq + 1)
                    stt(m.qf[:, nq % 2, :], PJ[:, 0:S], m.bq[:, 0:1], m.live[:, query, :], ALU.add, ALU.mult).then_inc(sem.qf_ok, 1)
                if on(done_):
                    need(count)
                    tt(m.s2[:, done_ % 3, :, 0:E], m.s1[:, nd % 2, :, 0:E], m.oh[:, nd % 2, 1, :, 0:E], ALU.add).then_inc(sem.oh_ok, 1)
                if on(query):
                    dve.wait_ge(sem.qh_ok, nq + 1)
                    tt(m.qr[:, nq % 2, :], m.qf[:, nq % 2, :] if L else PJ[:, 0:S], m.qh[:, nq % 2, :], ALU.subtract).then_inc(sem.qr_ok, 1)
                if on(scored):
                    maximum(L, scored, 2)
                if on(query):
                    dve.wait_ge(sem.qm_ok, nq + 1)
                    if nq >= 2:
                        dve.wait_ge(qst_in[(nq - 2) % 3], 16 * NP * ((nq - 2) // 3 + 1))
                    tt(m.ql[:, nq % 2, :], m.qr[:, nq % 2, :], m.qm[:, nq % 2, :], ALU.subtract).then_inc(sem.ql_ok, 1)
                if on(done_):
                    dve.wait_ge(sem.rank_ps, nd + 1)
                    tt(rt[:, :, :, 0:E], rank, m.oh[:, nd % 2, :, :, 0:E], ALU.mult).then_inc(sem.own_ok, 1)
                if on(scored):
                    maximum(L, scored, 3)
                if on(add):
                    x = m.x[:, 2 * add:2 * add + 2, :]
                    if L == 0:
                        dve.wait_ge(sem.pj_ps, add + 1)
                        dve.wait_ge(sem.xp_ok, add + 1)
                        more = PJ[:, 0:S].rearrange("p (t d) -> p t d", t=QT)
                    else:
                        dve.wait_ge(sem.att_ok, na + 1)
                        more = m.att[:, na % 2, :, :, :].rearrange("p (t c) h d -> p t (c h d)", t=QT)
                    tt(x, x, more, ALU.add).then_inc(sem.x1_ok, 1)
                if on(done_):
                    dve.wait_ge(sem.own_ok, nd + 1)
                    own = mark(dve.tensor_reduce(rk, rt[:, :, :, 0:E], AX.X, ALU.add))
                if on(add):
                    dve.wait_ge(sem.x1_ok, na + 1)
                    moment = moments(1, na, add)
                if on(done_):
                    need(own)
                    if L == 1:
                        ts(ro, rk, float(CAP), float(SKIP), ALU.is_ge, ALU.mult)
                    side = mark(tt(rb, rk, m.side[:, 0, :, :], ALU.mult))
                if on(add):
                    need(moment)
                    add_mv = mean_variance(1, na)
                if on(done_):
                    need(side)
                    side = mark(tt(rb, rb, m.side[:, 1 + L, :, :], ALU.add))
                v, p = halves(i), nf % 2
                if i <= B:
                    need(max(add_mv if on(add) else 0, fresh_mv if on(fresh) else 0))
                    ts(m.ve[:, v, p, :], m.mv[:, v, p, :, 1], EPS, None, ALU.add).then_inc(sem.var_ok, 1)
                if on(done_):
                    need(side)
                    dst, idx = m.slot[:, tiles, :], m.i8[:, tiles, 0:2]
                    if L == 0:
                        stt(dst, idx, float(REG0), rb, ALU.mult, ALU.add).then_inc(sem.slot_ok, 1)
                    else:
                        then(stt(slf, idx, float(REG1), rb, ALU.mult, ALU.add))
                        tt(dst, slf, ro, ALU.add).then_inc(sem.slot_ok, 1)
                if i <= B:
                    ve, g, u, tv, r = (x[:, v, p, :] for x in (m.ve, m.g, m.u, m.t, m.rs))
                    dve.wait_ge(sem.guess_ok, 12 * L + i + 4)
                    square = mark(tt(u, g, g, ALU.mult))
                if i <= B:
                    need(square)
                    then(stt(tv, u, -0.5, ve, ALU.mult, ALU.mult))
                    then(stt(r, tv, 1.5, g, ALU.add, ALU.mult))
                if on(add):
                    if add >= 2:
                        dve.wait_ge(sent[L][add % 2], 64 * (add // 2))
                    elif L == 1:
                        dve.wait_ge(sent[0][add], 16 * NT)
                    wait(dve, sem.xl_ps, na - 1)
                    for t in range(QT):
                        j = ts(m.xl[:, p, 0, t, 0:D], m.x[:, 2 * add + t, :], m.mv[:, 1, p, t, 0:1], m.rs[:, 1, p, t:t + 1],
                               ALU.subtract, ALU.mult)
                    j.then_inc(sem.xl_ok, 1)
                if on(fresh):
                    stt(m.shift[:, p, :], m.mv[:, 0, p, :, 0], -1.0, m.rs[:, 0, p, :], ALU.mult, ALU.mult).then_inc(sem.norm_ok, 1)

            def gates(L):
                v0, v1 = m.v8[:, :, 0], m.v8[:, :, 1]
                w0, w1 = m.wt[:, 0, :], m.wt[:, 1, :]
                if L == 1:
                    tt(m.wa[:], m.lg[:, :, 0:E1N], m.v8[:, :, 0:1].broadcast_to([P, NT, E1N]), ALU.subtract)
                tt(m.wd[:], v1, v0, ALU.subtract).then_inc(sem.gate_d, 1)
                dve.wait_ge(sem.gate_e, L + 1)
                if L == 0:
                    then(ts(m.wb[:], m.wc[:], 1.0, None, ALU.add))
                    then(dve.reciprocal(w0, m.wb[:]))
                    then(tt(w1, m.wc[:], w0, ALU.mult))
                else:
                    then(dve.tensor_reduce(m.wb[:], m.wa[:], AX.X, ALU.add))
                    then(dve.reciprocal(m.we[:], m.wb[:]))
                    then(tt(m.wc[:], m.wc[:], m.we[:], ALU.mult))
                    then(stt(m.wb[:], m.we[:], 1e-9, m.wc[:], ALU.add, ALU.add))
                    then(dve.reciprocal(m.wd[:], m.wb[:]))
                    tt(w0, m.we[:], m.wd[:], ALU.mult)
                    tt(w1, m.wc[:], m.wd[:], ALU.mult).then_inc(sem.weights_ok, 1)
                    dve.wait_ge(sem.weights_ok, 1)

            def table(L):
                dve.wait_ge(sem.cnt_ps, L + 1)
                E = EN[L]
                R = slice(0, NB0)
                then(copy(m.cnt[R, :, 0:E], PG[R, 0:2 * E].rearrange("p (k e) -> p k e", k=2)))
                c0, c1, ie = m.cnt[R, 0, 0:E], m.cnt[R, 1, 0:E], m.iota_e[R, 0:E]
                r = [m.tb[R, i, 0:E] for i in range(10)]
                if L == 1:
                    then(ts(r[0][0:1], c0[0:1], float(CAP), float(CAP), ALU.min, ALU.add))
                    stt(m.blk_r[0:1, 0:E], ie[0:1], float(REG1), r[0][0:1], ALU.mult, ALU.add).then_inc(sem.table_ok, 1)
                    return
                then(ts(r[0], c0, float(UP0), None, ALU.add))
                stt(m.pad_r[0:1, :], ie[0:1], float(REG0), r[0][0:1], ALU.mult, ALU.add).then_inc(sem.pad_ok, 1)
                dve.memset(r[2], 1.0)
                then(stt(m.toi[R, :], c0, float(P - 1), c1, ALU.add, ALU.add))
                stt(r[5], ie, float(REG0), c1, ALU.mult, ALU.subtract)
                then(ts(m.tot[R, :], m.toi[R, :], 7, None, ALU.logical_shift_right))
                then(copy(r[1], m.tot[R, :]))
                then(dve.tensor_tensor_scan(r[3], r[2], r[1], 0.0, ALU.mult, ALU.add))
                ts(r[7], r[3], m.number[R, 0:1], None, ALU.is_le)
                then(tt(r[4], r[3], r[1], ALU.subtract))
                dve.tensor_reduce(m.be[R, 0:1], r[7], AX.X, ALU.add)
                then(stt(r[6], r[4], float(-P), r[5], ALU.mult, ALU.add))
                ts(m.br[R, 0:1], m.be[R, 0:1], float(E0N), 1e8, ALU.is_ge, ALU.mult)
                then(stt(r[8], ie, m.be[R, 0:1], r[6], ALU.is_equal, ALU.mult))
                then(dve.tensor_reduce(m.bs[R, 0:1], r[8], AX.X, ALU.add))
                then(stt(m.bs[R, 1:2], m.number[R, :], float(P), m.bs[R, 0:1], ALU.mult, ALU.add))
                stt(m.br[R, 1:2], m.bs[R, 1:2], float(UP0), m.br[R, 0:1], ALU.add, ALU.add).then_inc(sem.row_ok, 1)
                dve.wait_ge(sem.row_ps, 1)
                ts(m.blk_r[:, 0:NB0], PG[0:1, NB0:2 * NB0], float(PAD0), None, ALU.min)
                ts(m.blk_e[:, 0:NB0], PG[0:1, 0:NB0], float(E0N - 1), None, ALU.min).then_inc(sem.table_ok, 1)

            order = [(iteration, None)]
            dve.wait_ge(sem.in_mask, 32)
            ts(m.pf[:], m.pi[:], 0.0, None, ALU.not_equal)
            ts(m.mf[:], m.mi[:], 0.0, None, ALU.not_equal).then_inc(sem.keep_ok, 1)
            split_keys(0)
            steps(0, order, end=-1)
            dve.wait_ge(sem.vb_ok, 1)
            split_values(0)
            dve.wait_ge(sem.in_const, 16 * 3)
            keys(0)
            copy(m.identb[:], m.ident[:])
            copy(m.upper[:], m.upperf[:])
            copy(m.sel[:].rearrange("p c k -> p (c k)"), m.self32[:]).then_inc(sem.sel_ok, 1)
            steps(0, order, first=-1, end=0)
            split_keys(1)
            split_values(1)
            dve.wait_ge(sem.in_small, 16 * 8)
            dve.wait_ge(sem.in_place, 16 * 5)
            tt(m.bgs[:], m.bg0[:, 0, :], m.bg0[:, 1, :], ALU.add)
            steps(0, order, first=0)
            table(0)
            dve.memset(m.s2[:, 2, :, :], 0.0)
            keys(1)
            gates(0)
            live_queries()

            def block_step(s, u, first=0, last=2):
                if first <= 0:
                    if s % 8 == 0:
                        expert.extend(eight(mybir.EngineType.DVE, m.blk_e, s, E0N - 1))
                    wait(dve, sem.bh_ps, s - 1)
                    copy(m.w1b[:, u % 2, :], m.w1_0[:, bass.ds(expert[s] * F0, F0)]).then_inc(sem.bw_ok, 1)
                    dve.wait_ge(sem.bx_ps, s + 1)
                    copy(m.place[:, s:s + 1], m.xb[:, u, D:ROW].bitcast(I32)).then_inc(sem.place_ok, 1)
                if first <= 2 <= last:
                    e = expert[s - 2]
                    v = (u - 2) % U
                    dve.wait_ge(sem.by_ps, s - 1)
                    wait(dve, back[0][v], (s - 2 - v) * (16 // U))
                    dve.tensor_tensor(m.yb[:, v, :], m.ps[6 + (u - 2) % 2][:, 0:D],
                                      m.b2_0[:, bass.ds(e * D, D)], ALU.add).then_inc(sem.by_ok, 1)

            dve.wait_ge(sem.in_ffn, 16 * 4 * B)
            dve.wait_ge(sem.table_ok, 1)
            expert = []
            for s in range(NB0 + 2):
                block_step(s, s % U, first=max(0, s - NB0 + 1), last=s)

            dve.wait_ge(sem.live_ok, 4)
            then(stt(m.mb[:], m.keep[:], 1.0, m.live[0:S2, :, :], ALU.subtract, ALU.mult))
            steps(1, order)
            table(1)
            gates(1)
            dve.wait_ge(sem.in_w1, 16 * (2 * E1N + 1))
            for e in range(E1N):
                dve.wait_ge(sem.ey_ps, e + 1)
                if e >= 4:
                    dve.wait_ge(back[1][e % 4], 32 * (e // 4))
                for t in range(2):
                    i = tt(m.yb[:, 2 * (e % 4) + t, :], [PJ, PG][e % 2][:, t * P:(t + 1) * P], m.b2_1[:, e * D:(e + 1) * D], ALU.add)
                i.then_inc(sem.ey_ok, 1)
            for b in range(B):
                dve.wait_ge(last_in[0][b // 2], 16)
                dve.wait_ge(sem.second_ok, b + 1)
                add_result(1, b, 0).then_inc(sem.xo_ok, 1)

        @block.scalar
        def _(act):
            fn = act.activation

            def copy(o, i):
                return fn(o, i, ACT.Copy)

            def guess(L, i):
                if i > B:
                    return
                v, p = halves(i), (B * L + i + 3) % 2
                act.wait_ge(sem.var_ok, 12 * L + i + 4)
                fn(m.ln[:, v, p, :], m.ve[:, v, p, :], ACT.Ln).then_inc(sem.a_step, 1)
                act.wait_ge(sem.a_step, 12 * L + i + 4)
                fn(m.g[:, v, p, :], m.ln[:, v, p, :], ACT.Exp, scale=-0.5).then_inc(sem.guess_ok, 1)

            def normal(L, b):
                n = B * L + b
                act.wait_ge(sem.norm_ok, n + 1)
                wait(act, sem.xn_ps, n - 1)
                for t in range(QT):
                    i = fn(m.xn[:, n % 2, t, :], m.x[:, 2 * b + t, :], ACT.Identity, scale=m.rs[:, 0, n % 2, t:t + 1],
                           bias=m.shift[:, n % 2, t:t + 1])
                i.then_inc(sem.xn_ok, 1)

            def xnT(L, b):
                n = B * L + b
                act.wait_ge(sem.xn_ps, n + 1)
                wait(act, sem.q_ps, n - 1)
                copy(m.xnT[:, n % 2, :], PM[:, 0:S]).then_inc(sem.xnT_ok, 1)

            def q_high(L, b):
                n = B * L + b
                act.wait_ge(sem.qf_ok if L else sem.q_ps, b + 1 if L else n + 1)
                if n >= 2:
                    act.wait_ge(qst_in[(n - 2) % 3], 16 * NP * ((n - 2) // 3 + 1))
                copy(m.qh[:, n % 2, :], m.qf[:, n % 2, :] if L else PJ[:, 0:S]).then_inc(sem.qh_ok, 1)

            def q_middle(L, b):
                n = B * L + b
                act.wait_ge(sem.qr_ok, n + 1)
                copy(m.qm[:, n % 2, :], m.qr[:, n % 2, :]).then_inc(sem.qm_ok, 1)

            def maxima(L, b):
                n = B * L + b
                act.wait_ge(sem.mx_ps, n + 1)
                wait(act, sem.t_ps, 4 * (n - 1))
                if L == 1:
                    copy(m.rm[0:S2, n % 2, :], m.mb[:, b, :])
                copy(m.rm[64:64 + H, n % 2, :], PG[:].bitcast(BF16)[64:64 + H, S:2 * S]).then_inc(sem.rm_ok, 1)

            def weights(L, b, u):
                n = B * L + b
                act.wait_ge(sem.t_ps, 4 * n + u + 1)
                if u == 0:
                    wait(act, sem.o_ps, n)
                fn(m.pT[:, 2 * u:2 * u + 2, :].rearrange("p c q -> p (c q)"), PT_[u % 2][:], ACT.Exp, scale=SCALE).then_inc(sem.pT_ok, 1)

            def sums(L, b):
                n = B * L + b
                act.wait_ge(sem.o_ps, n + 1)
                wait(act, sem.on_ps, n - 1)
                copy(m.oT[:, n % 2, :, :].rearrange("p g q -> p (g q)"), PO[:]).then_inc(sem.oT_ok, 1)

            def attT(L, b):
                act.wait_ge(sem.at_ps, b + 1)
                wait(act, sem.pj_ps, b - 1)
                copy(m.attT[:, b % 2, :], PM[:, 0:S]).then_inc(sem.attT_ok, 1)

            def xlT(L, b):
                n = B * L + b
                act.wait_ge(sem.xl_ps, n + 1)
                wait(act, sem.lg_ps, n - 1)
                copy(m.xlT[:, n % 2, :], PM[:, 0:S]).then_inc(sem.xlT_ok, 1)

            def order(L):
                return [(weights, 0, 0), (xnT, 2), (weights, 0, 1), (q_high, 2)] + ([(attT, -1)] if L == 0 else []) + [
                    (q_middle, 2), (weights, 0, 2), (weights, 0, 3), (maxima, 1), (guess, None), (sums, 0), (xlT, -1), (normal, 3)]

            def gates(L):
                act.wait_ge(sem.gate_d, L + 1)
                if L == 1:
                    fn(m.wa[:], m.wa[:], ACT.Exp)
                fn(m.wc[:], m.wd[:], ACT.Exp).then_inc(sem.gate_e, 1)

            act.preload_act_table_set("natural_log_exp_and_others")
            for dst, src in ((m.self32[:], a["c_sel"]), (m.hmask[:], a["c_hmask"]), (m.upperf[:], a["c_upper"])):
                act.dma_start(dst, src).then_inc(sem.in_const, 16)
            act.dma_start(m.mi[:], a["mask_1x1xSxS2_ik0"].rearrange("a b q k -> (a b q) k").rearrange("(t p) k -> p t k", p=P)).then_inc(sem.in_mask, 16)
            act.dma_start(m.pi[:], a["mask_Bx1x1xS2_ik0"]).then_inc(sem.in_mask, 16)
            act.wait_ge(sem.ctx_ok, 1)
            for h in range(2):
                i = copy(m.ctxD.rearrange("p b (h k) -> p b h k", h=2)[:, :, h, :], m.ctxT[:].rearrange("p (b k) -> p b k", b=B))
            i.then_inc(sem.ctxD_ok, 1)
            act.wait_ge(sem.sub_ps, 1)
            copy(m.subT[:], PG[0:S2, 0:S]).then_inc(sem.sub_ok, 1)
            steps(0, order(0))
            act.wait_ge(sem.pad_ok, 1)
            pads(act, mybir.EngineType.Activation, 8)
            gates(0)

            def block_step(s, u, first=0, last=1):
                if first <= 0:
                    act.wait_ge(sem.bx_ps, s + 1)
                    wait(act, sem.bh_ps, s - 1)
                    copy(m.xbT[:, u % 2, 0:P], m.ps[u % 2][:, 0:P]).then_inc(sem.bxT_ok, 1)
                if first <= 1 <= last:
                    if (s - 1) % 8 == 0:
                        expert.extend(eight(mybir.EngineType.Activation, m.blk_e, s - 1, E0N - 1))
                    e = expert[s - 1]
                    act.wait_ge(sem.bh_ps, s)
                    wait(act, sem.by_ps, s - 3)
                    for g in range(2):
                        i = fn(m.hT[:, (u - 1) % 2, g * P:(g + 1) * P], m.ps[2 + (u - 1) % 2][:, g * P:(g + 1) * P], ACT.Relu,
                               bias=m.b1_0[:, bass.ds(e, 1), g])
                    i.then_inc(sem.bh_ok, 1)

            act.wait_ge(sem.table_ok, 1)
            expert = []
            for s in range(NB0 + 1):
                block_step(s, s % U, first=max(0, s - NB0 + 1), last=s)

            steps(1, order(1))
            gates(1)
            act.preload_act_table_set("gelu_apprx_tanh_and_others")

            def expert_x(e):
                act.wait_ge(sem.ex_ps, e + 1)
                wait(act, sem.eh_ps, 4 * (e - 1))
                copy(m.xbT[:, e % 2, :], PM[:, 0:S]).then_inc(sem.exT_ok, 1)

            expert_x(0)
            for e in range(E1N):
                for g in range(4):
                    act.wait_ge(sem.eh_ps, 4 * e + g + 1)
                    if g == 0:
                        wait(act, sem.ey_ps, e - 1)
                    fn(m.hT[:, e % 2, g * S:(g + 1) * S], m.ps[g][:, 0:S], ACT.Gelu_apprx_tanh,
                       bias=m.b1_1[:, e, g:g + 1]).then_inc(sem.ehT_ok, 1)
                if e + 1 < E1N:
                    expert_x(e + 1)

            act.wait_ge(sem.weights_ok, 1)
            for b in range(B):
                act.wait_ge(last_in[1][b // 2], 16)
                for t in range(2 * b, 2 * b + 2):
                    i = fn(m.last[:, 1, t, :], m.last[:, 1, t, :], ACT.Copy, scale=m.wt[:, 1, t:t + 1])
                i.then_inc(sem.scaled, 1)

        @block.gpsimd
        def _(pool):
            def send(L):
                for b in range(B):
                    n = B * L + b
                    xl = m.xl[:, n % 2]
                    if L == 0 and b + 2 < B:
                        add_bias(b + 2)
                    pool.wait_ge(sem.xl_ok, n + 1)
                    pool.tensor_copy(xl[:, 1, :, 0:D], xl[:, 0, :, 0:D])
                    pool.tensor_copy(xl[:, :, :, D:ROW].bitcast(I32).rearrange("p k t o -> p k (t o)"),
                                     m.ids[:, 2 * b:2 * b + 2, :].rearrange("p t k -> p k t")).then_inc(sem.g_step, 1)
                    pool.wait_ge(sem.g_step, n + 1)
                    pool.wait_ge(sem.slot_ok, n + 1)
                    for t in range(QT):
                        for k in range(2):
                            pool.indirect_dma_start([xs0, xs1][L], bass.IndirectOffsetOnAxis(ap=m.slot[:, 2 * b + t, k:k + 1], axis=0),
                                                    xl[:, k, t, :], None, bounds_check=(PAD0 if L == 0 else E1N * REG1) - 1,
                                                    oob_is_err=False).then_inc(sent[L][n % 2], 16)

            last_place = pool.to_reg(2 * TOK - 1)

            def return_rows(L, rows, places, done):
                pool.indirect_dma_start(ys[L], bass.IndirectOffsetOnAxis(ap=places.bitcast(U32), axis=0), rows, None,
                                        bounds_check=last_place, oob_is_err=False).then_inc(done, 16)

            pool.memset(vb[0][:], 0.0)
            pool.memset(vb[1][:], 0.0).then_inc(sem.v0_ok, 1)
            pool.wait_ge(sem.v0_ok, 1)
            for v in vb:
                pool.memset(v[0:64, :, :, 16:17], 1.0)
                i = pool.memset(v[64:128, :, :, 17:18], 1.0)
            i.then_inc(sem.vb_ok, 1)
            pool.wait_ge(sem.vb_ok, 1)
            pool.memset(m.zero, 0.0).then_inc(sem.zero_ok, 1)
            pool.wait_ge(sem.keep_ok, 1)
            pool.wait_ge(sem.sub_ok, 1)
            for b in range(B):
                i = pool.tensor_scalar(m.keep[:, b, :], m.subT[:], m.pf[:, b:b + 1], None, ALU.mult)
            i.then_inc(sem.keep_ok, 1)
            pool.wait_ge(sem.in_place, 16 * 5)
            pool.wait_ge(sem.in_small, 16 * 8)

            def add_bias(b):
                pool.wait_ge(sem.xn_ok, b + 1)
                x = m.x[:, 2 * b:2 * b + 2, :]
                pool.tensor_tensor(x, x, m.bp[:].unsqueeze(1).broadcast_to([P, QT, D]), ALU.add).then_inc(sem.xp_ok, 1)

            add_bias(0)
            add_bias(1)
            send(0)
            for j in range(NB0):
                u = j % U
                pool.wait_ge(sem.by_ok, j + 1)
                return_rows(0, m.yb[:, u, :], m.place[:, j:j + 1], back[0][u])
            pool.wait_ge(sem.filled, 16 * (1 + E1N + 4))
            send(1)
            for e in range(E1N):
                pool.wait_ge(sem.ey_ok, e + 1)
                for t in range(2):
                    return_rows(1, m.yb[:, 2 * (e % 4) + t, :], m.xb[:, 2 * e + t, D:ROW], back[1][e % 4])
            for b in range(B):
                pool.wait_ge(sem.scaled, b + 1)
                x = m.x[:, 2 * b:2 * b + 2, :]
                pool.tensor_tensor(x, x, m.last[:, 1, 2 * b:2 * b + 2, :], ALU.add).then_inc(sem.second_ok, 1)


_DATA = ['x', 'ctx_1024', 'mask_Bx1x1xS2_ik0', 'mask_1x1xSxS2_ik0', 'L0_xattn_Wq', 'L0_xattn_Wk', 'L0_xattn_Wv', 'L0_xattn_Wp',
         'L0_xattn_bp', 'L0_ffn_Wg', 'L0_ffn_bg', 'L0_ffn_bias', 'L0_ffn_W1', 'L0_ffn_b1', 'L0_ffn_W2', 'L0_ffn_b2',
         'L1_xattn_Wq', 'L1_xattn_bq', 'L1_xattn_Wk', 'L1_xattn_bk', 'L1_xattn_Wv', 'L1_xattn_bv', 'L1_ffn_Wg', 'L1_ffn_W1',
         'L1_ffn_b1', 'L1_ffn_W2', 'L1_ffn_b2']


def constants():
    import numpy as np
    sel = np.zeros((80, NC, 2, S2), np.float32)
    for k in range(S2):
        sel[k, :, :, k] = MASK
    for h in range(H):
        sel[64 + h, h // 2, h % 2, :] = -1.0
    p = np.arange(P)
    hmask = np.zeros((KR, 2), np.float32)
    for r in range(KR):
        hmask[r, r % 16 // DH] = 1.0
    ids = (p[:, None, None] + P * np.arange(NT)[None, :, None] + TOK * np.arange(2)[None, None, :]).astype(np.int32)
    side = np.zeros((P, 3, QT, 2), np.float32)
    side[:, 0] = [1.0, -1.0]
    side[:, 1] = [UP0, UP0 - 1.0]
    side[:, 2] = [UP1, UP1 - 1.0]
    pad = np.zeros((P, 2, ROW), np.float32)
    pad.view(np.int32)[:, :, D] = SKIP
    return {"c_ident": np.eye(P, dtype=np.float32), "c_upper": np.triu(np.ones((P, P), np.float32), 1),
            "c_sel": sel.reshape(80, NC * P), "c_hmask": hmask,
            "c_iota": np.tile(np.arange(E0N, dtype=np.float32), (P, 1)), "c_ids": ids, "c_side": side,
            "c_pad": pad.reshape(P, 2 * ROW),
            "c_number": p.astype(np.float32).reshape(P, 1)}


def kernel(**inputs):
    import numpy as np
    import concourse.bacc as bacc
    from concourse.bass_utils import run_bass_kernel_spmd

    nc = bacc.Bacc("TRN2", target_bir_lowering=False, num_devices=1)
    data = {n: np.asarray(inputs[n]) for n in _DATA}
    for w in ("Wq", "Wk", "Wv"):
        data[f"L1_xattn_{w}"] = data[f"L1_xattn_{w}"].T
    for L in (0, 1):
        for w in ("Wq", "Wk"):
            data[f"L{L}_xattn_{w}"] = data[f"L{L}_xattn_{w}"].reshape(D, NC, 2 * DH).transpose(0, 2, 1).reshape(D, D)
    data["c_b1T0"] = data.pop("L0_ffn_b1").reshape(E0N, 2, P).transpose(2, 0, 1)
    data["c_b1T"] = data.pop("L1_ffn_b1").reshape(E1N, 4, P).transpose(2, 0, 1)
    for w in ("bq", "bk"):
        data[f"L1_xattn_{w}"] = data[f"L1_xattn_{w}"].reshape(NC, 2 * DH).T.reshape(P, 1)
    data["mask_Bx1x1xS2_ik0"] = data["mask_Bx1x1xS2_ik0"].reshape(B, S2).T
    data.update(constants())
    arrays = {f"in_{n}": np.ascontiguousarray(v) for n, v in data.items()}
    a = {n: nc.dram_tensor(f"in_{n}", arrays[f"in_{n}"].shape, mybir.dt.from_np(arrays[f"in_{n}"].dtype), kind="ExternalInput").ap()
         for n in data}
    out = nc.dram_tensor("out_0", (B, S, D), F32, kind="ExternalOutput").ap()
    mixture_kernel(nc, a, out)
    r = run_bass_kernel_spmd(nc, [arrays], core_ids=[0])
    return r.results[0]["out_0"]
```
